# Optimizing a Trainium2 kernel written in Bass

```python
import numpy as np
import jax
import jax.numpy as jnp

def _softmax(x, axis=-1):
    return jax.nn.softmax(x, axis=axis)

def _gelu(x):
    return jax.nn.gelu(x, approximate=True)

def _silu(x):
    return jax.nn.silu(x)

def _sigmoid(x):
    return jax.nn.sigmoid(x)

def _layernorm(x, axis=-1, eps=1e-05):
    m = jnp.mean(x, axis=axis, keepdims=True)
    v = jnp.var(x, axis=axis, keepdims=True)
    return (x - m) / jnp.sqrt(v + eps)

def _scatter_add(tgt, idx, src, axis=0):
    return tgt.at[idx].add(src)

def _segment_sum(src, seg, n):
    return jax.ops.segment_sum(src, seg, n)
kernel_name = 'mk_decoder_postln_d1_seqx_r4_6f8ad3'

def setup_inputs(seed: int=0):
    np.random.seed(seed)
    _w = jnp.asarray

    def _rec_inputs():
        import jax
        import jax.numpy as jnp
        _rk = jax.random.key(seed)
        x = -0.0005207 + 1.001 * jax.random.normal(jax.random.fold_in(_rk, 1), (1, 2048, 256), jnp.float32)
        _lenS = 2048 - jax.random.randint(jax.random.fold_in(_rk, 7), (1,), 0, max(1, 2048 // 4) + 1, jnp.int32)
        _lenS2 = 1601 - jax.random.randint(jax.random.fold_in(_rk, 8), (1,), 0, max(1, 1601 // 4) + 1, jnp.int32)
        _ctx_1024P = jax.random.normal(jax.random.fold_in(_rk, 11), (1, 16, 256), jnp.float32)
        _ctx_1024c = jax.random.dirichlet(jax.random.fold_in(_rk, 511), 0.3 * jnp.ones((16,), jnp.float32), (1, 1601))
        _ctx_1024t = jnp.einsum('bsk,bkd->bsd', _ctx_1024c, _ctx_1024P)
        _ctx_1024t = _ctx_1024t * jax.lax.rsqrt(jnp.mean(jnp.square(_ctx_1024t)) + 1e-12) * 0.953939
        ctx_1024 = 2.81802e-05 + 1.00001 * (_ctx_1024t + 0.3 * jax.random.normal(jax.random.fold_in(_rk, 611), (1, 1601, 256), jnp.float32))
        _validS = jnp.arange(2048)[None, :] < _lenS[:, None]
        _validS2 = jnp.arange(1601)[None, :] < _lenS2[:, None]
        _causal = jnp.tril(jnp.ones((2048, 2048), dtype=bool))
        mask_Bx1x1xS2_bf1 = jnp.ones((1, 1, 1, 1601), dtype=bool)
        return (x, ctx_1024, mask_Bx1x1xS2_bf1)
    x, ctx_1024, mask_Bx1x1xS2_bf1 = _rec_inputs()

    def _L0_attn_setup():
        import jax, jax.numpy as jnp
        import numpy as np
        import math
        DIM = 256
        NUM_HEADS = 16
        HEAD_DIM = DIM // NUM_HEADS
        MAX_BIAS = 8.0
        SCALE = HEAD_DIM ** (-0.5)

        def _alibi_slopes(n):

            def pow2(n):
                start = 2.0 ** (-2.0 ** (-(math.log2(n) - 3)))
                return [start * start ** i for i in range(n)]
            if math.log2(n).is_integer():
                return pow2(n)
            c = 2 ** math.floor(math.log2(n))
            return pow2(c) + _alibi_slopes(2 * c)[0::2][:n - c]

        def _rotate_half(t):
            t1, t2 = jnp.split(t, 2, axis=-1)
            return jnp.concatenate([-t2, t1], axis=-1)
        key = jax.random.key(seed)
        k1, k2, k3, k4 = jax.random.split(key, 4)
        B, N, C = (2, 512, DIM)
        x = jax.random.normal(k1, (B, N, C), dtype=jnp.float32)
        qkv_w = jax.random.normal(k2, (3 * C, C), dtype=jnp.float32) * C ** (-0.5)
        proj_w = jax.random.normal(k3, (C, C), dtype=jnp.float32) * C ** (-0.5)
        proj_b = jax.random.normal(k4, (C,), dtype=jnp.float32) * 0.01
        slopes = jnp.asarray(np.array(_alibi_slopes(NUM_HEADS), dtype=np.float32))
        return {'x': x, 'qkv_w': qkv_w, 'proj_w': proj_w, 'proj_b': proj_b, 'slopes': slopes}
    _L0_attn_all = _L0_attn_setup()
    _L0_attn_in = {k: v for k, v in _L0_attn_all.items() if k in ('qkv_w', 'proj_w', 'proj_b', 'slopes')}
    del _L0_attn_all

    def _L0_xattn_setup():
        import jax, jax.numpy as jnp
        import numpy as np
        D_MODEL = 256
        N_HEADS = 16
        D_HEAD = D_MODEL // N_HEADS

        def _split_heads(x):
            B, L, D = x.shape
            return x.reshape(B, L, N_HEADS, D_HEAD).transpose(0, 2, 1, 3)
        key = jax.random.key(seed)
        ks = jax.random.split(key, 6)
        B, LQ, LK = (4, 128, 1024)
        scale = 1.0 / np.sqrt(D_MODEL)
        return {'q_in': jax.random.normal(ks[0], (B, LQ, D_MODEL), dtype=jnp.float32), 'mem': jax.random.normal(ks[1], (B, LK, D_MODEL), dtype=jnp.float32), 'mem_mask': jnp.ones((B, 1, 1, LK), dtype=bool), 'Wq': jax.random.normal(ks[2], (D_MODEL, D_MODEL), dtype=jnp.float32) * scale, 'Wk': jax.random.normal(ks[3], (D_MODEL, D_MODEL), dtype=jnp.float32) * scale, 'Wv': jax.random.normal(ks[4], (D_MODEL, D_MODEL), dtype=jnp.float32) * scale, 'Wo': jax.random.normal(ks[5], (D_MODEL, D_MODEL), dtype=jnp.float32) * scale}
    _L0_xattn_all = _L0_xattn_setup()
    _L0_xattn_in = {k: v for k, v in _L0_xattn_all.items() if k in ('Wq', 'Wk', 'Wv', 'Wo')}
    del _L0_xattn_all

    def _L0_ffn_setup():
        import jax, jax.numpy as jnp
        import numpy as np
        TOP_K = 2
        key = jax.random.key(seed)
        ks = jax.random.split(key, 6)
        B, T, H, E, F = (2, 512, 256, 8, 1024)
        s = 0.02
        return {'hidden_states': jax.random.normal(ks[0], (B, T, H), dtype=jnp.float32), 'router_w': jax.random.normal(ks[1], (E, H), dtype=jnp.float32) * s, 'w1': jax.random.normal(ks[2], (E, F, H), dtype=jnp.float32) * s, 'b1': jax.random.normal(ks[3], (E, F), dtype=jnp.float32) * s, 'w2': jax.random.normal(ks[4], (E, H, F), dtype=jnp.float32) * s, 'b2': jax.random.normal(ks[5], (E, H), dtype=jnp.float32) * s}
    _L0_ffn_all = _L0_ffn_setup()
    _L0_ffn_in = {k: v for k, v in _L0_ffn_all.items() if k in ('router_w', 'w1', 'b1', 'w2', 'b2')}
    del _L0_ffn_all
    return {'x': x, 'ctx_1024': ctx_1024, 'mask_Bx1x1xS2_bf1': mask_Bx1x1xS2_bf1, 'L0_attn_qkv_w': _L0_attn_in['qkv_w'], 'L0_attn_proj_w': _L0_attn_in['proj_w'], 'L0_attn_proj_b': _L0_attn_in['proj_b'], 'L0_attn_slopes': _L0_attn_in['slopes'], 'L0_xattn_Wq': _L0_xattn_in['Wq'], 'L0_xattn_Wk': _L0_xattn_in['Wk'], 'L0_xattn_Wv': _L0_xattn_in['Wv'], 'L0_xattn_Wo': _L0_xattn_in['Wo'], 'L0_ffn_router_w': _L0_ffn_in['router_w'], 'L0_ffn_w1': _L0_ffn_in['w1'], 'L0_ffn_b1': _L0_ffn_in['b1'], 'L0_ffn_w2': _L0_ffn_in['w2'], 'L0_ffn_b2': _L0_ffn_in['b2']}

def reference(x, ctx_1024, mask_Bx1x1xS2_bf1, L0_attn_qkv_w, L0_attn_proj_w, L0_attn_proj_b, L0_attn_slopes, L0_xattn_Wq, L0_xattn_Wk, L0_xattn_Wv, L0_xattn_Wo, L0_ffn_router_w, L0_ffn_w1, L0_ffn_b1, L0_ffn_w2, L0_ffn_b2):
    import jax
    import jax.numpy as jnp

    def _L0_attn_ref(x, qkv_w, proj_w, proj_b, slopes):
        import jax, jax.numpy as jnp
        import numpy as np
        import math
        DIM = 256
        NUM_HEADS = 16
        HEAD_DIM = DIM // NUM_HEADS
        MAX_BIAS = 8.0
        SCALE = HEAD_DIM ** (-0.5)

        def _alibi_slopes(n):

            def pow2(n):
                start = 2.0 ** (-2.0 ** (-(math.log2(n) - 3)))
                return [start * start ** i for i in range(n)]
            if math.log2(n).is_integer():
                return pow2(n)
            c = 2 ** math.floor(math.log2(n))
            return pow2(c) + _alibi_slopes(2 * c)[0::2][:n - c]

        def _rotate_half(t):
            t1, t2 = jnp.split(t, 2, axis=-1)
            return jnp.concatenate([-t2, t1], axis=-1)
        B, N, C = x.shape
        H, D = (NUM_HEADS, HEAD_DIM)
        qkv = (x @ qkv_w.T).reshape(B, N, 3, H, D).transpose(2, 0, 3, 1, 4)
        q, k, v = (qkv[0], qkv[1], qkv[2])
        inv_freq = 1.0 / 10000.0 ** (jnp.arange(0, D, 2, dtype=jnp.float32) / D)
        freqs = jnp.arange(N, dtype=jnp.float32)[:, None] * inv_freq[None, :]
        sin = jnp.tile(jnp.sin(freqs), (1, 2))
        cos = jnp.tile(jnp.cos(freqs), (1, 2))
        q = q * cos + _rotate_half(q) * sin
        k = k * cos + _rotate_half(k) * sin
        attn = jnp.einsum('bhqd,bhkd->bhqk', q, k) * SCALE
        pos = jnp.arange(N, dtype=jnp.float32)
        diff = pos[None, :] - pos[:, None]
        diff = jnp.where(diff > 0, 0.0, diff)
        alibi = diff[None, :, :] * slopes[:, None, None] * MAX_BIAS
        attn = attn + alibi[None]
        w = jax.nn.softmax(attn, axis=-1)
        out = jnp.einsum('bhqk,bhkd->bhqd', w, v)
        out = out.transpose(0, 2, 1, 3).reshape(B, N, C)
        return out @ proj_w.T + proj_b

    def _L0_xattn_ref(q_in, mem, mem_mask, Wq, Wk, Wv, Wo):
        import jax, jax.numpy as jnp
        import numpy as np
        D_MODEL = 256
        N_HEADS = 16
        D_HEAD = D_MODEL // N_HEADS

        def _split_heads(x):
            B, L, D = x.shape
            return x.reshape(B, L, N_HEADS, D_HEAD).transpose(0, 2, 1, 3)
        q = _split_heads(q_in @ Wq.T)
        k = _split_heads(mem @ Wk.T)
        v = _split_heads(mem @ Wv.T)
        scores = jnp.einsum('bhqd,bhkd->bhqk', q, k) / jnp.sqrt(jnp.float32(D_HEAD))
        scores = jnp.where(mem_mask, scores, -jnp.inf)
        attn = jax.nn.softmax(scores, axis=-1)
        out = jnp.einsum('bhqk,bhkd->bhqd', attn, v)
        B, H, LQ, Dh = out.shape
        out = out.transpose(0, 2, 1, 3).reshape(B, LQ, H * Dh)
        return out @ Wo.T

    def _L0_ffn_ref(hidden_states, router_w, w1, b1, w2, b2):
        import jax, jax.numpy as jnp
        import numpy as np
        TOP_K = 2
        x = hidden_states
        router_logits = jnp.einsum('bth,eh->bte', x, router_w)
        topk_values, topk_indices = jax.lax.top_k(router_logits, TOP_K)
        topk_weights = jax.nn.softmax(topk_values.astype(jnp.float32), axis=-1).astype(x.dtype)
        h1 = jnp.einsum('bth,efh->btef', x, w1) + b1
        h1 = jax.nn.gelu(h1, approximate=False)
        expert_outputs = jnp.einsum('btef,ehf->bteh', h1, w2) + b2
        gather_idx = topk_indices[..., None]
        topk_expert_outputs = jnp.take_along_axis(expert_outputs, gather_idx, axis=2)
        mixed_output = jnp.sum(topk_expert_outputs * topk_weights[..., None], axis=2)
        return mixed_output
    x = _layernorm(x + _L0_attn_ref(x, L0_attn_qkv_w, L0_attn_proj_w, L0_attn_proj_b, L0_attn_slopes), axis=-1)
    x = _layernorm(x + _L0_xattn_ref(x, ctx_1024, mask_Bx1x1xS2_bf1, L0_xattn_Wq, L0_xattn_Wk, L0_xattn_Wv, L0_xattn_Wo), axis=-1)
    x = _layernorm(x + _L0_ffn_ref(x, L0_ffn_router_w, L0_ffn_w1, L0_ffn_b1, L0_ffn_w2, L0_ffn_b2), axis=-1)
    return x

_drawn_inputs = setup_inputs


def setup_inputs(seed=0):
    import zlib

    import numpy as np

    out = dict(_drawn_inputs(seed))
    spreads = {}
    factors = {'L0_attn_proj_b': 5.631, 'L0_ffn_b1': 8.0, 'L0_ffn_b2': 3.793}
    for name, (base, spread) in spreads.items():
        noise = np.random.default_rng([zlib.crc32(name.encode()), seed]).standard_normal(out[name].shape)
        drawn = base * np.exp(spread * noise) if base else spread * noise
        out[name] = jnp.asarray(drawn.astype(out[name].dtype))
    for name, factor in factors.items():
        out[name] = (out[name] * factor).astype(out[name].dtype)
    return out
```

```python
from contextlib import ExitStack

import concourse.bass as bass
from concourse import mybir
import numpy as np

ALU = mybir.AluOpType
ACT = mybir.ActivationFunctionType
AX = mybir.AxisListType
F32 = mybir.dt.float32
BF16 = mybir.dt.bfloat16
U8 = mybir.dt.uint8

P = 128
N = 2048
C = 256
CT = C // P
H = 16
D = C // H
NX = 1601
NXP = -(-NX // P) * P
TT = N // P
QB = 512
NQB = N // QB
E = 8
F = 1024
FT = F // P
PARTS = 3
PAIRS = 6
BIAS_ROWS = 12
MASK_ROW = 12
S0 = 13
A_ROWS = S0 + PAIRS * D
B_ROWS = A_ROWS + PARTS
RING = 3
PRING = 6
MASKED = -1.0e38
SCALE = float(D) ** -0.5
MAX_BIAS = 8.0
EPS = 1e-5
HEADS_LOOPED = 12


class Plan:

    def __init__(self, nk, keys):
        self.nk = nk
        self.keys = keys
        self.chunk = keys // 4
        self.nu = NQB * nk
        self.np = self.nu // 2
        self.nb = self.nu // 4
        self.max_slots = self.nb - (3 if nk == 16 else 2)
        self.last_batch = [((q + 1) * nk - 1) // 4 for q in range(NQB)]

    def ring_items(self, b, first, last):
        items = []
        for q in range(NQB):
            at = self.last_batch[q] + 3
            if at == b:
                items.append(("sum", q, 0))
            if at - self.nb == b and not first:
                items.append(("sum", q, -1))
        if not last:
            per = -(-4 * TT // self.max_slots)
            items += [("max", n // 4, n % 4) for n in range(per * b, min(per * (b + 1), 4 * TT))]
            if b == self.max_slots + 1:
                items.append(("shift", 0, 0))
        return items

    def saves(self, b, first):
        out = []
        for q in range(NQB):
            at = self.last_batch[q] + 2
            if at == b:
                out.append((q, 0))
            if at - self.nb == b and not first:
                out.append((q, -1))
        return out

    def ring_before(self, h):
        return 4 * TT + 2 + (4 * TT + 2 + NQB) * h - (0 if isinstance(h, int) and h == 0 else 1)


PROLOGUE = [("max", n // 4, n % 4) for n in range(4 * TT)] + [("shift", 0, 0)]
SELF = Plan(TT, N)
CROSS = Plan(NXP // P, NXP)


def width(item):
    return 2 if item[0] == "shift" else 1


def layer(nc, x, xT, ctxT, mask, wqkvT, wrotT, wpT, bp, slopes, xwqT, xwkT, xwvT, xwoT, rT, w1T, b1T, w2T, b2,
          cosT, sinT, constQ, constQX, constKL, constK0, ones3, ident, identb, dist, distT, sel, pick, out):
    with ExitStack() as ctx:
        def sb(name, shape, dt=F32):
            return ctx.enter_context(nc.sbuf_tensor(name, shape, dt))

        def ps(name, shape, dt=F32):
            return ctx.enter_context(nc.psum_tensor(name, shape, dt))

        def sem(name):
            return ctx.enter_context(nc.semaphore(name))

        X = sb("X", [P, TT, C])
        AT = sb("AT", [P, TT, C])
        XT = sb("XT", [P, CT, N])
        arena = sb("arena", [P, (TT + NXP // P) * C + CT * NXP])
        VA = arena[:, 0:TT * C].rearrange("p (t c) -> p t c", c=C)
        VX = arena[:, TT * C:(TT + NXP // P) * C].rearrange("p (t c) -> p t c", c=C)
        CX = arena[:, (TT + NXP // P) * C:].rearrange("p (k n) -> p k n", k=CT)
        HID = arena[:, 0:2 * FT * QB].rearrange("p (b f n) -> p b f n", b=2, f=FT)
        oper = sb("oper", [P, RING * 3 * N], BF16)
        QO = oper[:, 0:RING * N].rearrange("p (r n) -> p r n", r=RING)
        KO = oper[:, RING * N:].rearrange("p (r v n) -> p r v n", r=RING, v=2)
        wts = oper[:, 0:4 * 4 * F].bitcast(F32)
        W1 = wts[:, 0:2 * CT * F].rearrange("p (b k f) -> p b k f", b=2, k=CT)
        W2 = wts[:, 2 * CT * F:4 * CT * F].rearrange("p (b f c) -> p b f c", b=2, f=FT)
        PT = sb("PT", [P, PRING, 2, QB])
        flatPT = PT[:, :, :, :].rearrange("p a b c -> p (a b c)")
        cosS = flatPT[:, 0:N]
        sinS = flatPT[:, N:2 * N]
        OS = sb("OS", [P, 2, QB])
        VS = sb("VS", [P, RING, TT, 2 * D])
        SD = sb("SD", [P, RING, PARTS, P], BF16)
        flatAT = AT[:, :, :].rearrange("p t c -> p (t c)")
        T1 = flatAT[:, 0:2 * QB].rearrange("p (b n) -> p b n", b=2)
        T2 = flatAT[:, 2 * QB:4 * QB].rearrange("p (b n) -> p b n", b=2)
        slopeF = flatAT[0:6 * H, 4 * QB:4 * QB + N // 2].bitcast(BF16)
        QF = flatPT[:, 2 * N:2 * N + 3 * QB].rearrange("p (b n) -> p b n", b=3)
        RF = flatAT[:, 6 * QB:8 * QB].rearrange("p (b n) -> p b n", b=2)
        parts = sb("parts", [P, 3, PARTS, QB], BF16)
        wqkv = sb("wqkv", [P, CT, 3 * C])
        wrot = sb("wrot", [P, CT, 2 * C])
        wp = sb("wp", [P, CT, C])
        xwq = sb("xwq", [P, CT, C])
        xwk = sb("xwk", [P, CT, C])
        xwv = sb("xwv", [P, CT, C])
        xwo = sb("xwo", [P, CT, C])
        bpS = sb("bpS", [P, C])
        b2S = sb("b2S", [E, C])
        b1S = sb("b1S", [P, E * FT])
        b1E = sb("b1E", [P, 2, FT])
        rS = sb("rS", [P, CT, E])
        idf = sb("idf", [P, P])
        idb = sb("idb", [P, P], BF16)
        dS = sb("dS", [P, P], BF16)
        dTS = sb("dTS", [P, P], BF16)
        selS = sb("selS", [P, D + 1])
        slB = sb("slB", [P, H])
        sl8 = sb("sl8", [P, H])
        slP = sb("slP", [P, PARTS, H], BF16)
        slPF = sb("slPF", [P, PARTS, H])
        slR = sb("slR", [P, H])
        slopeDiag = sb("slopeDiag", [P, 2, PARTS, P], BF16)
        slRow = sb("slRow", [6 * H, 8])
        slRowB = sb("slRowB", [6 * H, 4], BF16)
        mU8 = sb("mU8", [1, NX], U8)
        mRow = sb("mRow", [1, NXP], BF16)
        CM = sb("CM", [P, TT, 4])
        NM = sb("NM", [P, TT])
        NR = sb("NR", [P, TT])
        SH = sb("SH", [P, PARTS, TT], BF16)
        MT = sb("MT", [PARTS * TT, P], BF16)
        RC = sb("RC", [P, 2, 4, 1])
        ATT = sb("ATT", [P, 2, CT, P])
        stats = sb("stats", [P, 2, 6])
        agg = sb("agg", [P, 2, 2])
        var = sb("var", [P, 2, 5])
        L = sb("L", [P, TT, E])
        G = sb("G", [P, TT, E])
        rank = sb("rank", [P, TT, E])
        cmp_ = sb("cmp_", [P, TT, E])
        beat = sb("beat", [P, TT, E])
        top = sb("top", [P, TT, 1])
        pickS = sb("pickS", [6 * H, PARTS])
        GT = PT[0:E, 0:2, :, :].rearrange("p a b c -> p (a b c)")

        S = [ps(f"S{i}", [P, 2, QB]) for i in range(2)]
        O = [ps(f"O{i}", [P, QB]) for i in range(2)]
        R = [ps(f"R{i}", [P, QB]) for i in range(2)]

        qD = nc.dram_tensor("qD", [PARTS, C, N], BF16).ap()
        kD = nc.dram_tensor("kD", [PARTS, C, N], BF16).ap()
        qxD = nc.dram_tensor("qxD", [PARTS, C, N], BF16).ap()
        kxD = nc.dram_tensor("kxD", [PARTS, C, NXP], BF16).ap()
        slD = nc.dram_tensor("slD", [6 * H, N], BF16).ap()
        sdD = nc.dram_tensor("sdD", [H * P, PARTS * P], BF16).ap()

        s_w = sem("weights_loaded")
        s_x = sem("stream_loaded")
        s_c = sem("context_loaded")
        s_k = sem("constants_loaded")
        s_rope = sem("rope_tables_loaded")
        s_m = sem("misc_constants_loaded")
        s_zero = sem("buffers_cleared")
        s_prep = sem("proj_ready")
        s_prepfree = sem("proj_read")
        s_chain = sem("prep_chain")
        s_q = sem("prep_value_ready")
        s_hi = sem("prep_high_ready")
        s_r = sem("prep_rest_ready")
        s_mi = sem("prep_middle_ready")
        s_lo = sem("prep_parts_ready")
        s_st = [sem(f"parts_stored{i}") for i in range(3)]
        s_v = sem("v_proj_ready")
        s_vs = sem("v_proj_saved")
        s_sl = sem("slope_chain")
        s_slout = sem("slope_rows_stored")
        s_sdr = sem("slope_diag_ready")
        s_sdo = [sem(f"slope_diag_stored{i}") for i in range(2)]
        s_mask = sem("mask_row_ready")
        s_mrow = sem("mask_row_placed")
        s_const = sem("constant_rows_placed")
        s_tr = sem("attention_transposed")
        s_att = sem("attention_transpose_saved")
        s_pj = sem("output_projected")
        s_ln = sem("norm_chain")
        s_var = sem("variance_ready")
        s_sd = sem("deviation_ready")
        s_xn = sem("stream_normed")
        s_xt = sem("stream_transposed")
        s_xts = sem("stream_transpose_saved")
        s_log = sem("logits_ready")
        s_gl = sem("logits_saved")
        s_gc = sem("gate_chain")
        s_ge = sem("gate_exp")
        s_g = sem("gates_ready")
        s_gt = sem("gates_transposed")
        s_gts = sem("gates_transpose_saved")
        s_b2 = sem("bias_mix_ready")
        s_acc0 = sem("experts_sum_started")
        s_w1 = [sem(f"w1_loaded{i}") for i in range(2)]
        s_w2 = [sem(f"w2_loaded{i}") for i in range(2)]
        s_hid = sem("hidden_ready")
        s_gelu = sem("gelu_done")
        s_b1 = sem("expert_bias_ready")
        s_moe = sem("expert_ready")
        s_moef = sem("expert_added")
        s_out = sem("output_stored")

        class Att:
            def __init__(self, name):
                self.loaded = [sem(f"{name}_operands_loaded{i}") for i in range(RING)]
                self.shift_loaded = sem(f"{name}_shift_loaded")
                self.scores = sem(f"{name}_scores_ready")
                self.exps = sem(f"{name}_exps_done")
                self.pv = sem(f"{name}_pv_done")
                self.saved = sem(f"{name}_acc_saved")
                self.filled = sem(f"{name}_ring_filled")
                self.freed = sem(f"{name}_ring_freed")
                self.sums = sem(f"{name}_sums_taken")
                self.v = sem(f"{name}_v_staged")
                self.chain = sem(f"{name}_shift_chain")
                self.cols = sem(f"{name}_shift_cols_ready")
        SA, XA = Att("self"), Att("cross")

        block = ctx.enter_context(nc.Block())

        def items_of(kind, n):
            return [(kind, half, c * n, n) for half in range(CT) for c in range(4)]
        PREP1 = items_of("q", QB) + items_of("k", QB) + items_of("xk", NXP // 4)
        PREP2 = items_of("xq", QB)
        dest = {"q": qD, "k": kD, "xk": kxD, "xq": qxD}
        NPREP = len(PREP1)

        def head_steps(engine, body):
            body(0, 0, 0)
            with engine.Fori(0, HEADS_LOOPED // RING) as it:
                for c in range(RING):
                    h = it * RING + (1 + c)
                    body(h, (1 + c) % RING, it + (1 + c) // RING)
            for h in range(HEADS_LOOPED + 1, H):
                body(h, h % RING, h // RING)

        @block.sync
        def _(sp):
            sp.dma_start(XT[:, :, :], xT.rearrange("(k p) n -> p k n", p=P)).then_inc(s_x, 16)
            sp.dma_start(wqkv[:, :, :], wqkvT.rearrange("(k p) n -> p k n", p=P)).then_inc(s_w, 16)
            sp.dma_start(wrot[:, :, :], wrotT.rearrange("(k p) n -> p k n", p=P)).then_inc(s_w, 16)
            sp.dma_start(cosS, cosT).then_inc(s_rope, 16)
            sp.dma_start(sinS, sinT).then_inc(s_rope, 16)
            sp.dma_start(CX[:, :, 0:NX], ctxT.rearrange("(k p) n -> p k n", p=P)).then_inc(s_c, 16)
            for w, src in ((xwk, xwkT), (xwv, xwvT), (xwq, xwqT), (wp, wpT), (xwo, xwoT)):
                sp.dma_start(w[:, :, :], src.rearrange("(k p) n -> p k n", p=P)).then_inc(s_c, 16)
            sp.dma_start(X[:, :, :], x.rearrange("(t p) c -> p t c", p=P)).then_inc(s_m, 16)
            sp.dma_start(bpS[:, :], bp.partition_broadcast(P)).then_inc(s_m, 16)
            sp.dma_start(b2S[:, :], b2).then_inc(s_m, 16)
            sp.dma_start(b1S[:, :], b1T).then_inc(s_m, 16)
            sp.dma_start(rS[:, :, :], rT.rearrange("(k p) n -> p k n", p=P)).then_inc(s_m, 16)
            for r in range(RING):
                sp.dma_start(QO[0:S0, r, :], constQ).then_inc(s_const, 16)
                sp.dma_start(KO[0:S0, r, 0, :], constKL).then_inc(s_const, 16)
                sp.dma_start(KO[0:S0, r, 1, :], constK0).then_inc(s_const, 16)
                for v in range(2):
                    sp.dma_start(KO[A_ROWS:B_ROWS, r, v, :], ones3).then_inc(s_const, 16)

            def store_parts(items, first):
                for n, (kind, half, c0, w) in enumerate(items):
                    i = first + n
                    sp.wait_ge(s_lo, i + 1)
                    sp.dma_start(dest[kind][:, half * P:(half + 1) * P, c0:c0 + w].rearrange("s r c -> r s c"),
                                 parts[:, i % 3, :, 0:w]).then_inc(s_st[i % 3], 16)

            sp.wait_ge(s_sl, 1)
            sp.dma_start(slD, slopeF).then_inc(s_slout, 16)
            for h in range(H):
                sp.wait_ge(s_sdr, h + 1)
                sp.dma_start(sdD[h * P:(h + 1) * P, :], slopeDiag[:, h % 2, :, :].rearrange("p s j -> p (s j)")).then_inc(s_sdo[h % 2], 16)
            store_parts(PREP1, 0)
            for i in range(3):
                sp.wait_ge(s_st[i], 16 * (NPREP // 3))
            sp.wait_ge(s_slout, 16)
            sp.wait_ge(s_sdo[0], 16 * H // 2)
            sp.wait_ge(s_sdo[1], 16 * H // 2)
            sp.wait_ge(s_const, 16 * 5 * RING)

            def attention_loads(A, plan, qsrc, ksrc):
                alibi = A is SA

                def load(h, c):
                    rows = bass.ds(h * D, D)
                    q = QO[S0:A_ROWS, c, :]
                    ld = A.loaded[c]
                    sp.dma_start(q[0:3 * D, :], qsrc[0:3, rows, :]).then_inc(ld, 16)
                    sp.dma_start(q[3 * D:5 * D, :], qsrc[0:2, rows, :]).then_inc(ld, 16)
                    sp.dma_start(q[5 * D:6 * D, :], qsrc[0, rows, :]).then_inc(ld, 16)
                    for v in range(2 if alibi else 1):
                        k = KO[S0:A_ROWS, c, v, 0:plan.keys]
                        row = 0
                        for part, times in ((0, 3), (1, 2), (2, 1)):
                            sp.dma_start(k[row:row + times * D, :],
                                         ksrc[part:part + 1, rows, :].to_broadcast([times, D, plan.keys])).then_inc(ld, 16)
                            row += times * D
                    if alibi:
                        srows = bass.ds(h * 6, 6)
                        sp.dma_start(QO[0:BIAS_ROWS:2, c, :], slD[srows, :]).then_inc(ld, 16)
                        sp.dma_start(KO[1:BIAS_ROWS:2, c, 0, :], slD[srows, :]).then_inc(ld, 16)
                        sp.dma_start(SD[:, c, :, :].rearrange("p s j -> p (s j)"), sdD[bass.ds(h * P, P), :]).then_inc(ld, 16)

                def place_shift(h, c):
                    sp.wait_ge(A.freed, plan.ring_before(h))
                    for s in range(PARTS):
                        sp.dma_start(QO[A_ROWS + s:A_ROWS + s + 1, c, :],
                                     MT[s * TT:(s + 1) * TT, :]).then_inc(A.shift_loaded, 16)

                for h in range(RING):
                    load(h, h)
                place_shift(0, 0)

                def step(h, c, turn):
                    whole = isinstance(h, int)
                    if not (whole and (h == 0 or h + 2 >= H)):
                        sp.wait_ge(A.scores, plan.np * h)
                        load(h + 2, (c + 2) % RING)
                    if not (whole and h + 1 >= H):
                        place_shift(h + 1, (c + 1) % RING)
                head_steps(sp, step)

            attention_loads(SA, SELF, qD, kD)
            sp.wait_ge(SA.scores, SELF.np * H)
            for r in range(RING):
                sp.dma_start(QO[0:S0, r, :], constQX).then_inc(s_mrow, 16)
                sp.dma_start(KO[0:BIAS_ROWS, r, 0, :], constK0[0:BIAS_ROWS, :]).then_inc(s_mrow, 16)
                if r == 0:
                    sp.wait_ge(s_mask, 2)
                sp.dma_start(KO[MASK_ROW:MASK_ROW + 1, r, 0, 0:NXP], mRow[:, :]).then_inc(s_mrow, 16)
            store_parts(PREP2, NPREP)
            for i in range(3):
                sp.wait_ge(s_st[i], 16 * ((NPREP + len(PREP2) - i + 2) // 3))
            attention_loads(XA, CROSS, qxD, kxD)

            def load_w1(e, b):
                sp.dma_start(W1[:, b, :, :], w1T[bass.ds(e * C, C), :].rearrange("(k p) f -> p k f", p=P)).then_inc(s_w1[b], 16)

            def load_w2(e, b):
                sp.dma_start(W2[:, b, :, :], w2T[bass.ds(e * F, F), :].rearrange("(f p) c -> p f c", p=P)).then_inc(s_w2[b], 16)
            sp.wait_ge(XA.scores, CROSS.np * H)
            for e in range(2):
                load_w1(e, e)
                load_w2(e, e)
            with sp.Fori(0, E // 2 - 1) as it:
                for b in range(2):
                    e = it * 2 + b
                    sp.wait_ge(s_hid, e * (4 * FT) + 4 * FT)
                    load_w1(e + 2, b)
                    sp.wait_ge(s_moe, e * TT + TT + 8)
                    load_w2(e + 2, b)
            for t in range(TT):
                sp.wait_ge(s_xn, 2 * TT + t + 1)
                sp.dma_start(out[t * P:(t + 1) * P, :], X[:, t, :]).then_inc(s_out, 16)
            sp.wait_ge(s_out, 16 * TT)

        @block.gpsimd
        def _(pool):
            pool.dma_start(slB[:, :], slopes.partition_broadcast(P)).then_inc(s_k, 16)
            pool.dma_start(slRow[:, 0:1],
                           slopes.rearrange("(h s o) -> h s o", s=1, o=1).to_broadcast([H, 6, 1])).then_inc(s_k, 16)
            pool.dma_start(mU8[:, :], mask).then_inc(s_k, 16)
            for dst, src in ((idf, ident), (idb, identb), (dS, dist), (dTS, distT), (selS, sel), (pickS, pick)):
                pool.dma_start(dst[:, :], src).then_inc(s_k, 16)
            pool.memset(CX[:, :, NX:NXP], 0.0).then_inc(s_zero, 1)
            pool.memset(VS[:, :, :, D:2 * D], 0.0).then_inc(s_zero, 1)
            pool.wait_ge(s_zero, 2)
            pool.memset(VS[:, :, :, D:D + 1], 1.0).then_inc(s_zero, 1)

            def stage(A, plan, V):
                nk = plan.nk

                def step(h, c, turn):
                    if not (isinstance(h, int) and h < RING):
                        pool.wait_ge(A.pv, plan.nb * (h - RING + 1))
                    pool.tensor_copy(VS[:, c, 0:nk, 0:D], V[:, 0:nk, bass.ds(h * D, D)]).then_inc(A.v, 1)
                step(0, 0, 0)
                step(1, 1, 0)
                step(2, 2, 0)
                with pool.Fori(1, H // RING) as it:
                    for c in range(RING):
                        step(it * RING + c, c, it)
                for h in range(H // RING * RING, H):
                    step(h, h % RING, h // RING)
            pool.wait_ge(s_vs, TT)
            stage(SA, SELF, VA)
            pool.wait_ge(s_vs, TT + NXP // P)
            pool.wait_ge(SA.pv, SELF.nb * H)
            stage(XA, CROSS, VX)

        @block.tensor
        def _(pe):
            def prep(items, first):
                for n, (kind, half, c0, w) in enumerate(items):
                    i = first + n
                    wt, off = {"q": (wqkv, 0), "k": (wqkv, C), "xk": (xwk, 0), "xq": (xwq, 0)}[kind]
                    src = CX if kind == "xk" else XT
                    if i >= 2:
                        pe.wait_ge(s_prepfree, i - 1)
                    for k in range(CT):
                        mm = pe.matmul(S[i % 2][:, 0, 0:w], wt[:, k, off + half * P:off + (half + 1) * P],
                                       src[:, k, c0:c0 + w], start=(k == 0), stop=(k == CT - 1))
                    if kind in "qk":
                        for k in range(CT):
                            mm = pe.matmul(S[i % 2][:, 1, 0:w], wrot[:, k, off + half * P:off + (half + 1) * P],
                                           src[:, k, c0:c0 + w], start=(k == 0), stop=(k == CT - 1))
                    mm.then_inc(s_prep, 1)

            def v_proj(src, wt, off, n, first):
                for t in range(n):
                    i = first + t
                    if i >= 2:
                        pe.wait_ge(s_vs, i - 1)
                    for k in range(CT):
                        mm = pe.matmul(R[i % 2][:, 0:C], src[:, k, t * P:(t + 1) * P], wt[:, k, off:off + C],
                                       start=(k == 0), stop=(k == CT - 1))
                    mm.then_inc(s_v, 1)

            pe.wait_ge(s_x, 16)
            pe.wait_ge(s_w, 32)
            prep(PREP1[0:16], 0)
            v_proj(XT, wqkv, 2 * C, TT, 0)
            pe.wait_ge(s_c, 16 * 6)
            pe.wait_ge(s_zero, 3)
            prep(PREP1[16:], 16)
            v_proj(CX, xwv, 0, NXP // P, TT)

            def attention(A, plan):
                alibi = A is SA
                nk, ch = plan.nk, plan.chunk

                def ring_item(item, pos, bank, h, c):
                    kind, a, b = item
                    if kind == "shift":
                        pe.wait_ge(A.freed, pos)
                    elif not isinstance(pos, int) or pos >= 2:
                        pe.wait_ge(A.freed, pos - 1)
                    slot = R[bank % 2]
                    if kind == "max":
                        t, k0, k1 = a, b * ch, (b + 1) * ch
                        c2 = (c + 1) % RING
                        if a == 0 and b == 0:
                            pe.wait_ge(A.loaded[c2], loads_due(h, c2))
                        q = QO[0:A_ROWS, c2, t * P:(t + 1) * P]
                        low = min(max(t * P, k0), k1) - k0 if alibi else ch
                        diag = alibi and k0 <= t * P < k1
                        if low:
                            mm = pe.matmul(slot[:, 0:low], q, KO[0:A_ROWS, c2, 0, k0:k0 + low],
                                           start=True, stop=True, skip_group_check=True)
                        if low < ch:
                            mm = pe.matmul(slot[:, low:ch], q, KO[0:A_ROWS, c2, 1, k0 + low:k1],
                                           start=(low == 0), stop=not diag, skip_group_check=True)
                        if diag:
                            for s in range(PARTS):
                                mm = pe.matmul(slot[:, low:low + P], SD[:, c2, s, :], dS[:, :],
                                               start=False, stop=(s == PARTS - 1), skip_group_check=True)
                        mm.then_inc(A.filled, 1)
                    elif kind == "shift":
                        pe.wait_ge(A.cols, h + 2)
                        pe.transpose(slot[0:PARTS * TT, 0:P // 2].bitcast(BF16), SH[:, :, :].rearrange("p s t -> p (s t)"),
                                     idb[:, :]).then_inc(A.filled, 2)
                    else:
                        pe.wait_ge(A.saved, (h + b) * NQB + (a + 1))
                        for t in range(4):
                            mm = pe.matmul(slot[:, t * 32:t * 32 + D + 1], OS[:, a % 2, t * P:(t + 1) * P], selS[:, :],
                                           start=True, stop=True, skip_group_check=True)
                        mm.then_inc(A.filled, 1)

                def loads_due(h, c2):
                    per = 16 * (12 if alibi else 6)
                    if isinstance(h, int):
                        return per * ((h + 1) // RING + 1)
                    return turn_now[0] * per

                turn_now = [None]

                def scores_unit(u, h, c):
                    qb, kt = u // nk, u % nk
                    bank = S[(c * plan.np + u // 2) % 2][:, u % 2, :]
                    q0 = qb * QB
                    lo = min(max(kt * P - q0, 0), QB) if alibi else 0
                    diag = alibi and q0 <= kt * P < q0 + QB
                    up = lo + P if diag else lo
                    stat = [KO[0:B_ROWS, c, v, kt * P:(kt + 1) * P] for v in range(2)]
                    if up:
                        mm = pe.matmul(bank[:, 0:up], stat[1], QO[0:B_ROWS, c, q0:q0 + up],
                                       start=True, stop=not diag, skip_group_check=True)
                    if diag:
                        for s in range(PARTS):
                            mm = pe.matmul(bank[:, lo:up], SD[:, c, s, :], dTS[:, :],
                                           start=False, stop=(s == PARTS - 1), skip_group_check=True)
                    if up < QB:
                        mm = pe.matmul(bank[:, up:QB], stat[0], QO[0:B_ROWS, c, q0 + up:q0 + QB],
                                       start=(up == 0), stop=True, skip_group_check=True)
                    return mm

                def pv_batch(b, h, c):
                    pe.wait_ge(A.exps, plan.np * h + (2 * b + 2))
                    for u in range(4 * b, 4 * b + 4):
                        qb, kt = u // nk, u % nk
                        if kt == 0 and not (isinstance(h, int) and h == 0 and qb < 2):
                            pe.wait_ge(A.saved, h * NQB + (qb - 1))
                        g = kt % 4
                        mm = pe.matmul(O[qb % 2][32 * g:32 * g + 32, :], VS[:, c, kt, :],
                                       PT[:, (c * plan.np + u // 2) % PRING, u % 2, :],
                                       start=(kt < 4), stop=(kt + 4 >= nk), skip_group_check=True)
                    mm.then_inc(A.pv, 1)

                def step(h, c, turn):
                    whole = isinstance(h, int)
                    first, last = whole and h == 0, whole and h == H - 1
                    turn_now[0] = turn + (1 if c == RING - 1 else 0) + 1
                    pos = plan.ring_before(h)
                    static = plan.ring_before(0 if first else 1)
                    pe.wait_ge(A.shift_loaded, (h + 1) * 16 * PARTS)
                    off = 0
                    for b in range(plan.nb):
                        items = plan.ring_items(b, first, last)
                        cut = -(-len(items) // 2)
                        for half in range(2):
                            p = 2 * b + half
                            if not (first and p < 2):
                                pe.wait_ge(A.exps, plan.np * h + (p - 1))
                            scores_unit(2 * p, h, c)
                            scores_unit(2 * p + 1, h, c).then_inc(A.scores, 1)
                            for item in (items[:cut], items[cut:])[half]:
                                ring_item(item, pos + off, static + off, h, c)
                                off += width(item)
                        if b == 0:
                            if not first:
                                pv_batch(plan.nb - 1, h - 1, (c - 1) % RING)
                            pe.wait_ge(A.v, h + 1)
                        else:
                            pv_batch(b - 1, h, c)

                pos = 0
                for item in PROLOGUE:
                    ring_item(item, pos, pos, -1, RING - 1)
                    pos += width(item)
                head_steps(pe, step)
                pv_batch(plan.nb - 1, H - 1, (H - 1) % RING)
                end = plan.ring_before(H) - (4 * TT + 2)
                for q in range(NQB):
                    if plan.last_batch[q] + 3 >= plan.nb:
                        ring_item(("sum", q, 0), end, end, H - 1, 0)
                        end += 1

            def project_norm(call, A, plan, w):
                pe.wait_ge(A.freed, plan.ring_before(H) - (4 * TT + 2) + 1)
                b0 = call * TT
                for s in range(TT + 3):
                    if s < TT:
                        if s >= 2:
                            pe.wait_ge(s_att, b0 + s - 1)
                        for k in range(CT):
                            mm = pe.transpose(S[0][:, s % 2, k * P:(k + 1) * P], AT[:, s, k * P:(k + 1) * P], idf[:, :])
                        mm.then_inc(s_tr, 1)
                    t = s - 1
                    if 0 <= t < TT:
                        pe.wait_ge(s_att, b0 + t + 1)
                        if t >= 2:
                            pe.wait_ge(s_xn, b0 + t - 1)
                        for k in range(CT):
                            mm = pe.matmul(S[1][:, t % 2, 0:C], ATT[:, t % 2, k, :], w[:, k, :],
                                           start=(k == 0), stop=(k == CT - 1))
                        mm.then_inc(s_pj, 1)
                    t = s - 3
                    if 0 <= t < TT:
                        pe.wait_ge(s_xn, b0 + t + 1)
                        if t >= 2:
                            pe.wait_ge(s_xts, b0 + t - 1)
                        for k in range(CT):
                            mm = pe.transpose(O[t % 2][:, k * P:(k + 1) * P], X[:, t, k * P:(k + 1) * P], idf[:, :])
                        mm.then_inc(s_xt, 1)

            pe.wait_ge(s_prepfree, NPREP)
            pe.wait_ge(s_vs, TT + NXP // P)
            pe.wait_ge(s_k, 16 * 9)
            pe.wait_ge(s_const, 16 * 5 * RING)
            attention(SA, SELF)
            project_norm(0, SA, SELF, wp)
            pe.wait_ge(s_xts, TT)
            pe.wait_ge(s_xn, TT)
            prep(PREP2, NPREP)
            pe.wait_ge(s_prepfree, NPREP + len(PREP2))
            pe.wait_ge(s_mrow, 16 * 3 * RING)
            attention(XA, CROSS)
            project_norm(1, XA, CROSS, xwo)

            pe.wait_ge(s_xts, 2 * TT)
            for t in range(TT):
                for k in range(CT):
                    mm = pe.matmul(R[0][:, t * E:(t + 1) * E], XT[:, k, t * P:(t + 1) * P], rS[:, k, :],
                                   start=(k == 0), stop=(k == CT - 1), skip_group_check=True)
            mm.then_inc(s_log, 1)
            pe.wait_ge(s_g, 1)
            for t in range(TT):
                mm = pe.transpose(S[t // 8][0:E, t // 4 % 2, (t % 4) * P:(t % 4 + 1) * P], G[:, t, :], idf[:, :])
            mm.then_inc(s_gt, 1)
            pe.wait_ge(s_gts, 4)
            for t in range(TT):
                if t >= 2:
                    pe.wait_ge(s_acc0, t - 1)
                pe.matmul(O[t % 2][:, 0:C], GT[:, t * P:(t + 1) * P], b2S[:, :], start=True, stop=True).then_inc(s_b2, 1)
            pe.wait_ge(s_acc0, TT)

            HB = [S[0][:, 0, :], S[0][:, 1, :], S[1][:, 0, :], S[1][:, 1, :]]
            OB = [O[0], O[1], R[0], R[1]]
            pe.sem_inc(s_gelu, 4)
            pe.sem_inc(s_moe, 8)
            pe.sem_inc(s_moef, 4)

            def first_layer(e, b, tb):
                for f in range(FT):
                    n = tb * FT + f
                    pe.wait_ge(s_gelu, e * (4 * FT) + n + 1)
                    for k in range(CT):
                        mm = pe.matmul(HB[f % 4], W1[:, b, k, f * P:(f + 1) * P], XT[:, k, tb * QB:(tb + 1) * QB],
                                       start=(k == 0), stop=(k == CT - 1))
                    mm.then_inc(s_hid, 1)

            def second_layer(e, b, tb):
                pe.wait_ge(s_gelu, e * (4 * FT) + (tb + 1) * FT + 4)
                for j in range(4):
                    pe.wait_ge(s_moef, e * TT + tb * 4 + j + 1)
                    for f in range(FT):
                        mm = pe.matmul(OB[j][:, 0:C], HID[:, tb % 2, f, j * P:(j + 1) * P], W2[:, b, f, :],
                                       start=(f == 0), stop=(f == FT - 1))
                    mm.then_inc(s_moe, 1)

            with pe.Fori(0, E // 2) as it:
                for b in range(2):
                    e = it * 2 + b
                    pe.wait_ge(s_w1[b], it * 16 + 16)
                    first_layer(e, b, 0)
                    pe.wait_ge(s_w2[b], it * 16 + 16)
                    for tb in range(1, 4):
                        first_layer(e, b, tb)
                        second_layer(e, b, tb - 1)
                    second_layer(e, b, 3)

        @block.scalar
        def _(act):
            def prep(items, first):
                n = len(items)
                for s in range(n + 1):
                    if s < n:
                        i, w = first + s, items[s][3]
                        act.wait_ge(s_q, i + 1)
                        if i >= 3:
                            act.wait_ge(s_st[i % 3], 16 * (i // 3))
                        act.activation(parts[:, i % 3, 0, 0:w], QF[:, i % 3, 0:w], ACT.Copy).then_inc(s_hi, 1)
                    if s >= 1:
                        i, w = first + s - 1, items[s - 1][3]
                        act.wait_ge(s_r, i + 1)
                        act.activation(parts[:, i % 3, 1, 0:w], RF[:, i % 2, 0:w], ACT.Copy).then_inc(s_mi, 1)

            def v_save(V, n, first):
                for t in range(n):
                    i = first + t
                    act.wait_ge(s_v, i + 1)
                    act.activation(V[:, t, :], R[i % 2][:, 0:C], ACT.Copy).then_inc(s_vs, 1)

            prep(PREP1[0:16], 0)
            v_save(VA, TT, 0)
            prep(PREP1[16:], 16)
            v_save(VX, NXP // P, TT)

            def attention(A, plan):
                def save(q, h):
                    act.wait_ge(A.pv, plan.nb * h + (plan.last_batch[q] + 1))
                    if not (isinstance(h, int) and h == 0 and q < 2):
                        act.wait_ge(A.sums, h * NQB + (q - 1))
                    act.activation(OS[:, q % 2, :], O[q % 2][:, :], ACT.Copy).then_inc(A.saved, 1)

                def step(h, c, turn):
                    first = isinstance(h, int) and h == 0
                    for b in range(plan.nb):
                        for p in (2 * b, 2 * b + 1):
                            act.wait_ge(A.scores, plan.np * h + (p + 1))
                            if not (first and p < PRING):
                                act.wait_ge(A.pv, plan.nb * h + (p // 2 - PRING // 2 + 1))
                            act.activation(PT[:, (c * plan.np + p) % PRING, :, :], S[(c * plan.np + p) % 2][:, :, :],
                                           ACT.Exp).then_inc(A.exps, 1)
                            if p % 2 == 0:
                                for q, back in plan.saves(b, first):
                                    save(q, h + back)
                head_steps(act, step)
                for q in range(NQB):
                    if plan.last_batch[q] + 2 >= plan.nb:
                        save(q, H - 1)

            def root(i):
                act.wait_ge(s_var, i + 1)
                act.activation(var[:, i % 2, 1:2], var[:, i % 2, 0:1], ACT.Sqrt).then_inc(s_sd, 1)

            def transposes(call):
                b0 = call * TT
                for s in range(TT + 3):
                    if s < TT:
                        act.wait_ge(s_tr, b0 + s + 1)
                        if s >= 2:
                            act.wait_ge(s_pj, b0 + s - 1)
                        act.activation(ATT[:, s % 2, :, :].rearrange("p k j -> p (k j)"), S[0][:, s % 2, 0:C],
                                       ACT.Copy).then_inc(s_att, 1)
                    if 1 <= s <= TT:
                        root(b0 + s - 1)
                    t = s - 3
                    if t >= 0:
                        act.wait_ge(s_xt, b0 + t + 1)
                        act.activation(XT[:, :, t * P:(t + 1) * P], O[t % 2][:, 0:C].rearrange("p (k j) -> p k j", k=CT),
                                       ACT.Copy).then_inc(s_xts, 1)

            attention(SA, SELF)
            transposes(0)
            prep(PREP2, NPREP)
            attention(XA, CROSS)
            transposes(1)
            act.wait_ge(s_gc, 2)
            act.activation(G[:, :, :], cmp_[:, :, :], ACT.Exp).then_inc(s_ge, 1)
            act.wait_ge(s_gt, 1)
            for j in range(4):
                act.activation(GT[:, j * QB:(j + 1) * QB], S[j // 2][0:E, j % 2, :], ACT.Copy).then_inc(s_gts, 1)
            HB = [S[0][:, 0, :], S[0][:, 1, :], S[1][:, 0, :], S[1][:, 1, :]]
            with act.Fori(0, E // 2) as it:
                for b in range(2):
                    e = it * 2 + b
                    act.activation(b1E[:, b, :], b1S[:, bass.ds(e * FT, FT)], ACT.Copy).then_inc(s_b1, 1)
                    act.wait_ge(s_b1, e + 1)
                    for tb in range(4):
                        act.wait_ge(s_moe, e * TT + tb * 4 + 4)
                        for f in range(FT):
                            act.wait_ge(s_hid, e * (4 * FT) + tb * FT + f + 1)
                            act.activation(HID[:, tb % 2, f, :], HB[f % 4], ACT.Gelu,
                                           bias=b1E[:, b, f:f + 1]).then_inc(s_gelu, 1)
            for t in range(TT):
                root(2 * TT + t)

        @block.vector
        def _(dve):
            links = {}

            def link(ins, s):
                links[s] = links.get(s, 0) + 1
                ins.then_inc(s, 1)
                dve.wait_ge(s, links[s])

            dve.wait_ge(s_k, 16 * 9)
            link(dve.memset(slopeF, 1.0), s_chain)
            link(dve.tensor_scalar(slRow[:, 1:2], slRow[:, 0:1], MAX_BIAS, None, ALU.mult), s_chain)
            link(dve.tensor_copy(slRowB[:, 0:1], slRow[:, 1:2]), s_chain)
            link(dve.tensor_tensor(slRow[:, 2:3], slRow[:, 1:2], slRowB[:, 0:1], ALU.subtract), s_chain)
            link(dve.tensor_copy(slRowB[:, 1:2], slRow[:, 2:3]), s_chain)
            link(dve.tensor_tensor(slRowB[:, 2:3], slRow[:, 2:3], slRowB[:, 1:2], ALU.subtract), s_chain)
            link(dve.tensor_tensor(slRow[:, 3:6], slRowB[:, 0:3], pickS[:, :], ALU.mult), s_chain)
            link(dve.tensor_reduce(slRow[:, 6:7], slRow[:, 3:6], AX.X, ALU.add), s_chain)
            dve.tensor_scalar(slopeF, slopeF, slRow[:, 6:7], None, ALU.mult).then_inc(s_sl, 1)
            link(dve.tensor_scalar(sl8[:, :], slB[:, :], MAX_BIAS, None, ALU.mult), s_chain)
            link(dve.tensor_copy(slP[:, 0, :], sl8[:, :]), s_chain)
            link(dve.tensor_tensor(slR[:, :], sl8[:, :], slP[:, 0, :], ALU.subtract), s_chain)
            link(dve.tensor_copy(slP[:, 1, :], slR[:, :]), s_chain)
            link(dve.tensor_tensor(slP[:, 2, :], slR[:, :], slP[:, 1, :], ALU.subtract), s_chain)
            link(dve.tensor_copy(slPF[:, :, :], slP[:, :, :]), s_chain)
            for h in range(H):
                if h >= 2:
                    dve.wait_ge(s_sdo[h % 2], 16 * (h // 2))
                for s in range(PARTS):
                    ins = dve.tensor_scalar(slopeDiag[:, h % 2, s, :], idf[:, :], slPF[:, s, h:h + 1], None, ALU.mult)
                ins.then_inc(s_sdr, 1)
            link(dve.memset(mRow[:, :], MASKED), s_mask)
            dve.tensor_scalar(mRow[:, 0:NX], mU8[:, :], -1.0, -MASKED, ALU.add, ALU.mult).then_inc(s_mask, 1)
            dve.wait_ge(s_m, 16 * 5)
            link(dve.tensor_tensor(X[:, :, :], X[:, :, :], bpS[:, :].unsqueeze(1).to_broadcast([P, TT, C]), ALU.add), s_chain)

            def prep(items, first):
                n = len(items)
                for s in range(n + 2):
                    if s < n:
                        i = first + s
                        kind, half, c0, w = items[s]
                        dve.wait_ge(s_prep, i + 1)
                        if i >= 3:
                            dve.wait_ge(s_r, i - 2)
                        if kind in "qk":
                            if i >= 2:
                                dve.wait_ge(s_q, i - 1)
                            dve.tensor_tensor(T1[:, i % 2, 0:w], S[i % 2][:, 0, 0:w], cosS[:, c0:c0 + w], ALU.mult)
                            ins = dve.tensor_tensor(T2[:, i % 2, 0:w], S[i % 2][:, 1, 0:w], sinS[:, c0:c0 + w], ALU.mult)
                            ins.then_inc(s_prepfree, 1)
                            dve.wait_ge(s_prepfree, i + 1)
                            dve.tensor_tensor(QF[:, i % 3, 0:w], T1[:, i % 2, 0:w], T2[:, i % 2, 0:w], ALU.add).then_inc(s_q, 1)
                        else:
                            dve.tensor_scalar(QF[:, i % 3, 0:w], S[i % 2][:, 0, 0:w], SCALE if kind == "xq" else 1.0, None,
                                              ALU.mult).then_inc(s_prepfree, 1)
                            dve.wait_ge(s_prepfree, i + 1)
                            dve.sem_inc(s_q, 1)
                    if 1 <= s <= n:
                        i, w = first + s - 1, items[s - 1][3]
                        dve.wait_ge(s_hi, i + 1)
                        if i >= 2:
                            dve.wait_ge(s_lo, i - 1)
                        dve.tensor_tensor(RF[:, i % 2, 0:w], QF[:, i % 3, 0:w], parts[:, i % 3, 0, 0:w], ALU.subtract).then_inc(s_r, 1)
                    if s >= 2:
                        i, w = first + s - 2, items[s - 2][3]
                        dve.wait_ge(s_mi, i + 1)
                        dve.tensor_tensor(parts[:, i % 3, 2, 0:w], RF[:, i % 2, 0:w], parts[:, i % 3, 1, 0:w], ALU.subtract).then_inc(s_lo, 1)

            dve.wait_ge(s_rope, 32)
            prep(PREP1[0:16], 0)
            prep(PREP1[16:], 16)

            def attention(A, plan):
                ch = plan.chunk

                def ring_item(item, pos, bank, h):
                    kind, a, b = item
                    slot = R[bank % 2]
                    if kind == "max":
                        dve.wait_ge(A.filled, pos + 1)
                        dve.tensor_reduce(CM[:, a, b:b + 1], slot[:, 0:ch], AX.X, ALU.max).then_inc(A.freed, 1)
                        if (a, b) == (TT - 1, 3):
                            n = (h + 1) * 4
                            dve.wait_ge(A.freed, pos + 1)
                            dve.tensor_reduce(NM[:, :], CM[:, :, :], AX.X, ALU.max, negate=True).then_inc(A.chain, 1)
                            dve.wait_ge(A.chain, n + 1)
                            dve.tensor_copy(SH[:, 0, :], NM[:, :]).then_inc(A.chain, 1)
                            dve.wait_ge(A.chain, n + 2)
                            dve.tensor_tensor(NR[:, :], NM[:, :], SH[:, 0, :], ALU.subtract).then_inc(A.chain, 1)
                            dve.wait_ge(A.chain, n + 3)
                            dve.tensor_copy(SH[:, 1, :], NR[:, :]).then_inc(A.chain, 1)
                            dve.wait_ge(A.chain, n + 4)
                            dve.tensor_tensor(SH[:, 2, :], NR[:, :], SH[:, 1, :], ALU.subtract).then_inc(A.cols, 1)
                    elif kind == "shift":
                        dve.wait_ge(A.filled, pos + 2)
                        if not (isinstance(h, int) and h < 0):
                            dve.wait_ge(A.shift_loaded, (h + 1) * (16 * PARTS))
                        dve.tensor_copy(MT[:, :], slot[0:PARTS * TT, 0:P // 2].bitcast(BF16)).then_inc(A.freed, 2)
                    else:
                        dve.wait_ge(A.filled, pos + 1)
                        g = (h + b) * NQB + a
                        v = slot[:, 0:P].rearrange("p (t j) -> p t j", j=32)
                        dve.reciprocal(RC[:, a % 2, :, :], v[:, :, D:D + 1]).then_inc(A.sums, 1)
                        dve.wait_ge(A.sums, g + 1)
                        dve.tensor_tensor(AT[:, 4 * a:4 * a + 4, bass.ds((h + b) * D, D)], v[:, :, 0:D],
                                          RC[:, a % 2, :, :].to_broadcast([P, 4, D]), ALU.mult).then_inc(A.freed, 1)

                def step(h, c, turn):
                    whole = isinstance(h, int)
                    first, last = whole and h == 0, whole and h == H - 1
                    pos, bank, off = plan.ring_before(h), plan.ring_before(0 if first else 1), 0
                    for b in range(plan.nb):
                        for item in plan.ring_items(b, first, last):
                            ring_item(item, pos + off, bank + off, h)
                            off += width(item)
                pos = 0
                for item in PROLOGUE:
                    ring_item(item, pos, pos, -1)
                    pos += width(item)
                head_steps(dve, step)
                end = plan.ring_before(H) - (4 * TT + 2)
                for q in range(NQB):
                    if plan.last_batch[q] + 3 >= plan.nb:
                        ring_item(("sum", q, 0), end, end, H - 1)
                        end += 1

            def norms(call):
                for s in range(TT + 1):
                    if s < TT:
                        b = s % 2
                        y = X[:, s, :] if call < 2 else AT[:, s, :]
                        if call < 2:
                            dve.wait_ge(s_pj, call * TT + s + 1)
                            link(dve.tensor_tensor(y, S[1][:, b, 0:C], y, ALU.add), s_ln)
                        link(dve.bn_stats(stats[:, b, :], y), s_ln)
                        link(dve.bn_aggr(agg[:, b, :], stats[:, b, :]), s_ln)
                        dve.tensor_scalar(var[:, b, 0:1], agg[:, b, 1:2], EPS, None, ALU.add).then_inc(s_var, 1)
                    if s >= 1:
                        t, b = s - 1, (s - 1) % 2
                        y = X[:, t, :] if call < 2 else AT[:, t, :]
                        dve.wait_ge(s_sd, call * TT + t + 1)
                        link(dve.reciprocal(var[:, b, 2:3], var[:, b, 1:2]), s_ln)
                        link(dve.scalar_tensor_tensor(out=var[:, b, 3:4], in0=var[:, b, 2:3], scalar=var[:, b, 2:3],
                                                      in1=var[:, b, 0:1], op0=ALU.mult, op1=ALU.mult), s_ln)
                        link(dve.tensor_scalar(var[:, b, 3:4], var[:, b, 3:4], -0.5, 1.5, ALU.mult, ALU.add), s_ln)
                        link(dve.tensor_tensor(var[:, b, 4:5], var[:, b, 2:3], var[:, b, 3:4], ALU.mult), s_ln)
                        dve.tensor_scalar(X[:, t, :], y, agg[:, b, 0:1], var[:, b, 4:5], ALU.subtract, ALU.mult).then_inc(s_xn, 1)

            attention(SA, SELF)
            norms(0)
            prep(PREP2, NPREP)
            attention(XA, CROSS)
            norms(1)

            gc = [0]

            def glink(ins):
                gc[0] += 1
                ins.then_inc(s_gc, 1)
                dve.wait_ge(s_gc, gc[0])
            dve.wait_ge(s_log, 1)
            dve.tensor_copy(L[:, :, :], R[0][:, 0:TT * E].rearrange("p (t e) -> p t e", e=E)).then_inc(s_gl, 1)
            dve.wait_ge(s_gl, 1)
            glink(dve.tensor_reduce(top[:, :, 0], L[:, :, :], AX.X, ALU.max))
            glink(dve.tensor_tensor(cmp_[:, :, :], L[:, :, :], top[:, :, :].to_broadcast([P, TT, E]), ALU.subtract))
            glink(dve.memset(rank[:, :, :], 0.0))
            for j in range(E):
                lj = L[:, :, j:j + 1]
                if j + 1 < E:
                    glink(dve.tensor_tensor(beat[:, :, j + 1:E], lj.to_broadcast([P, TT, E - 1 - j]), L[:, :, j + 1:E], ALU.is_ge))
                glink(dve.tensor_tensor(beat[:, :, 0:j + 1], lj.to_broadcast([P, TT, j + 1]), L[:, :, 0:j + 1], ALU.is_gt))
                glink(dve.tensor_tensor(rank[:, :, :], rank[:, :, :], beat[:, :, :], ALU.add))
            glink(dve.tensor_scalar(rank[:, :, :], rank[:, :, :], 2.0, None, ALU.is_lt))
            dve.wait_ge(s_ge, 1)
            glink(dve.tensor_tensor(G[:, :, :], G[:, :, :], rank[:, :, :], ALU.mult))
            glink(dve.tensor_reduce(top[:, :, 0], G[:, :, :], AX.X, ALU.add))
            glink(dve.reciprocal(top[:, :, :], top[:, :, :]))
            dve.tensor_tensor(G[:, :, :], G[:, :, :], top[:, :, :].to_broadcast([P, TT, E]), ALU.mult).then_inc(s_g, 1)

            for t in range(TT):
                dve.wait_ge(s_b2, t + 1)
                dve.tensor_tensor(AT[:, t, :], O[t % 2][:, 0:C], X[:, t, :], ALU.add).then_inc(s_acc0, 1)
            dve.wait_ge(s_acc0, TT)
            dve.wait_ge(s_g, 1)
            OB = [O[0], O[1], R[0], R[1]]
            with dve.Fori(0, E) as e:
                for t in range(TT):
                    dve.wait_ge(s_moe, e * TT + (t + 1 + 8))
                    dve.scalar_tensor_tensor(out=AT[:, t, :], in0=OB[t % 4][:, 0:C], scalar=G[:, t, bass.ds(e, 1)],
                                             in1=AT[:, t, :], op0=ALU.mult, op1=ALU.add).then_inc(s_moef, 1)
            dve.wait_ge(s_moef, 4 + E * TT)
            norms(2)


def _tables():
    def bf(v):
        return (np.ascontiguousarray(v, dtype=np.float32).view(np.uint32) >> 16).astype(np.uint16)
    pos = np.arange(N)
    inv = (np.float32(1.0) / np.float32(10000.0) ** (np.arange(0, D, 2, dtype=np.float32) / np.float32(D))).astype(np.float32)
    freqs = (pos.astype(np.float32)[:, None] * inv[None, :]).astype(np.float32)
    cos, sin = np.cos(freqs).T, np.sin(freqs).T
    root = np.float32(SCALE ** 0.5)
    cosT = np.tile(np.concatenate([cos, cos]), (P // D, 1)).astype(np.float32) * root
    sinT = np.tile(np.concatenate([-sin, sin]), (P // D, 1)).astype(np.float32) * root
    hi, lo = pos // P * P, pos % P
    q = np.zeros((S0, N), np.float32)
    kl = np.zeros((S0, N), np.float32)
    for s in range(PARTS):
        q[4 * s + 1], q[4 * s + 3] = -hi, -lo
        kl[4 * s], kl[4 * s + 2] = hi, lo
    q[MASK_ROW] = 1.0
    qx = np.zeros((S0, N), np.float32)
    qx[MASK_ROW] = 1.0
    sel = np.zeros((P, D + 1), np.float32)
    for g in range(4):
        sel[32 * g + np.arange(D + 1), np.arange(D + 1)] = 1.0
    j = np.arange(P)
    dist = np.minimum(j[None, :] - j[:, None], 0)
    pick = np.zeros((6 * H, PARTS), np.float32)
    pick[np.arange(6 * H), np.arange(6 * H) % 6 // 2] = 1.0
    return {
        "cosT": cosT, "sinT": sinT, "constQ": bf(q), "constQX": bf(qx), "constKL": bf(kl),
        "constK0": bf(np.zeros((S0, N))), "ones3": bf(np.ones((PARTS, N))), "ident": np.eye(P, dtype=np.float32),
        "identb": bf(np.eye(P)), "dist": bf(dist), "distT": bf(dist.T), "sel": sel, "pick": pick,
    }


def kernel(**inputs):
    import concourse.bacc as _bacc
    from concourse.bass_utils import run_bass_kernel_spmd as _run

    i = {k: np.asarray(v) for k, v in inputs.items()}
    qkv = i["L0_attn_qkv_w"]
    rot = np.arange(2 * C).reshape(-1, 2, D // 2)[:, ::-1].reshape(-1)
    a = {
        "x": i["x"][0], "xT": i["x"][0].T, "ctxT": i["ctx_1024"][0].T,
        "mask": i["mask_Bx1x1xS2_bf1"].reshape(1, NX).view(np.uint8),
        "wqkvT": qkv.T, "wrotT": qkv[rot].T, "wpT": i["L0_attn_proj_w"].T, "bp": i["L0_attn_proj_b"],
        "slopes": i["L0_attn_slopes"], "xwqT": i["L0_xattn_Wq"].T, "xwkT": i["L0_xattn_Wk"].T,
        "xwvT": i["L0_xattn_Wv"].T, "xwoT": i["L0_xattn_Wo"].T, "rT": i["L0_ffn_router_w"].T,
        "w1T": i["L0_ffn_w1"].transpose(0, 2, 1).reshape(E * C, F),
        "b1T": i["L0_ffn_b1"].reshape(E * FT, P).T,
        "w2T": i["L0_ffn_w2"].transpose(0, 2, 1).reshape(E * F, C), "b2": i["L0_ffn_b2"],
    }
    a.update(_tables())
    nc = _bacc.Bacc("TRN2", target_bir_lowering=False, num_devices=1)
    arrays, aps = {}, {}
    for name, v in a.items():
        v = np.ascontiguousarray(v)
        arrays[f"in_{name}_dram"] = v
        aps[name] = nc.dram_tensor(f"in_{name}_dram", v.shape, mybir.dt.from_np(v.dtype), kind="ExternalInput").ap()
        if v.dtype == np.uint16:
            aps[name] = aps[name].bitcast(BF16)
    aps["out"] = nc.dram_tensor("out_0_dram", (1, N, C), F32, kind="ExternalOutput").ap().rearrange("o n c -> (o n) c")
    layer(nc, **aps)
    r = _run(nc, [arrays], core_ids=[0])
    return r.results[0]["out_0_dram"]
```

```python
from contextlib import ExitStack

import concourse.bass as bass
from concourse import mybir
import numpy as np

ALU = mybir.AluOpType
ACT = mybir.ActivationFunctionType
AX = mybir.AxisListType
F32 = mybir.dt.float32
BF16 = mybir.dt.bfloat16
U8 = mybir.dt.uint8

P = 128
N = 2048
C = 256
CT = C // P
H = 16
D = C // H
NX = 1601
NXP = -(-NX // P) * P
TT = N // P
QB = 512
NQB = N // QB
E = 8
F = 1024
FT = F // P
PARTS = 3
PAIRS = 6
BIAS_ROWS = 12
MASK_ROW = 12
S0 = 13
A_ROWS = S0 + PAIRS * D
B_ROWS = A_ROWS + PARTS
LEAD = 3
RING = 3
PRING = 12
SBANKS = 3
RBANKS = 3
MASKED = -1.0e38
SCALE = float(D) ** -0.5
MAX_BIAS = 8.0
EPS = 1e-5
HEADS_LOOPED = 12


class Plan:

    def __init__(self, nk, keys):
        self.nk = nk
        self.keys = keys
        self.chunk = keys // 4
        self.nu = NQB * nk
        self.nb = self.nu // 4
        self.last_batch = [((q + 1) * nk - 1) // 4 for q in range(NQB)]
        self.per = -(-4 * TT // self.nb)
        self.early = min(LEAD * self.per, 4 * TT)
        self.prologue = self.chunks(0, 4 * TT, 1) + [("shift", 0, 0, 1)] + self.chunks(0, self.early, 2)

    def chunks(self, first, end, ahead):
        return [("max", n // 4, n % 4, ahead) for n in range(first, end)]

    def ring_items(self, b, h):
        whole = isinstance(h, int)
        items = []
        for q in range(NQB):
            at = self.last_batch[q] + 3
            if at == b:
                items.append(("sum", q, 0, 0))
            if at - self.nb == b and not (whole and h == 0):
                items.append(("sum", q, 0, -1))
        slot = b + LEAD
        if slot < self.nb:
            if not (whole and h + 1 >= H):
                items += self.chunks(self.per * slot, min(self.per * (slot + 1), 4 * TT), 1)
        elif not (whole and h + 2 >= H):
            slot -= self.nb
            items += self.chunks(self.per * slot, self.per * (slot + 1), 2)
        if b == self.nb - LEAD + 1 and not (whole and h + 1 >= H):
            items.insert(2, ("shift", 0, 0, 1))
        return items

    def saves(self, b, first):
        out = []
        for q in range(NQB):
            at = self.last_batch[q] + 2
            if at == b:
                out.append((q, 0))
            if at - self.nb == b and not first:
                out.append((q, -1))
        return out

    def used(self, items):
        return sum(width(i) for i in items)

    def head_items(self, h):
        return [i for b in range(self.nb) for i in self.ring_items(b, h)]

    def ring_before(self, h):
        if isinstance(h, int):
            return self.used(self.prologue) + sum(self.used(self.head_items(g)) for g in range(h))
        each = self.used(self.head_items(1))
        return h * each + (self.ring_before(1) - each)

    def static_before(self, h, c):
        assert RING * self.used(self.head_items(1)) % RBANKS == 0
        return self.ring_before(h if isinstance(h, int) else (c if c else RING))

    def shift_end(self, h):
        if isinstance(h, int) and h == 0:
            return 4 * TT + 1
        before = h - 1
        items = self.head_items(before if isinstance(before, int) else 1)
        at = [i[0] for i in items].index("shift")
        return self.ring_before(before) + self.used(items[:at + 1])


def width(item):
    return 1


SELF = Plan(TT, N)
CROSS = Plan(NXP // P, NXP)


def layer(nc, x, xT, ctxT, mask, wqkvT, wrotT, wpT, bp, slopes, xwqT, xwkT, xwvT, xwoT, rT, w1T, b1T, w2T, b2,
          cosT, sinT, constQ, constQX, constKL, constK0, ones3, ident, identb, dist, distT, sel, pick, out):
    with ExitStack() as ctx:
        def sb(name, shape, dt=F32):
            return ctx.enter_context(nc.sbuf_tensor(name, shape, dt))

        def ps(name, shape, dt=F32):
            return ctx.enter_context(nc.psum_tensor(name, shape, dt))

        def sem(name):
            return ctx.enter_context(nc.semaphore(name))

        X = sb("X", [P, TT, C])
        AT = sb("AT", [P, TT, C])
        XT = sb("XT", [P, CT, N])
        arena = sb("arena", [P, (TT + NXP // P) * C + CT * NXP])
        VA = arena[:, 0:TT * C].rearrange("p (t c) -> p t c", c=C)
        VX = arena[:, TT * C:(TT + NXP // P) * C].rearrange("p (t c) -> p t c", c=C)
        CX = arena[:, (TT + NXP // P) * C:].rearrange("p (k n) -> p k n", k=CT)
        HID = arena[:, 0:2 * FT * QB].rearrange("p (b f n) -> p b f n", b=2, f=FT)
        oper = sb("oper", [P, RING * 3 * N], BF16)
        QO = oper[:, 0:RING * N].rearrange("p (r n) -> p r n", r=RING)
        KO = oper[:, RING * N:].rearrange("p (r v n) -> p r v n", r=RING, v=2)
        wts = oper[:, 0:4 * 4 * F].bitcast(F32)
        W1 = wts[:, 0:2 * CT * F].rearrange("p (b k f) -> p b k f", b=2, k=CT)
        W2 = wts[:, 2 * CT * F:4 * CT * F].rearrange("p (b f c) -> p b f c", b=2, f=FT)
        PT = sb("PT", [P, PRING, QB])
        flatPT = PT[:, :, :].rearrange("p a b -> p (a b)")
        cosS = flatPT[:, 0:N]
        sinS = flatPT[:, N:2 * N]
        OS = sb("OS", [P, 2, QB])
        VS = sb("VS", [P, RING, TT, 2 * D])
        SD = sb("SD", [P, RING, PARTS, P], BF16)
        flatAT = AT[:, :, :].rearrange("p t c -> p (t c)")
        T1 = flatAT[:, 0:2 * QB].rearrange("p (b n) -> p b n", b=2)
        T2 = flatAT[:, 2 * QB:4 * QB].rearrange("p (b n) -> p b n", b=2)
        slopeF = flatAT[0:6 * H, 4 * QB:4 * QB + N // 2].bitcast(BF16)
        QF = flatPT[:, 2 * N:2 * N + 3 * QB].rearrange("p (b n) -> p b n", b=3)
        RF = flatAT[:, 6 * QB:8 * QB].rearrange("p (b n) -> p b n", b=2)
        parts = sb("parts", [P, 3, PARTS, QB], BF16)
        wqkv = sb("wqkv", [P, CT, 3 * C])
        wrot = sb("wrot", [P, CT, 2 * C])
        wp = sb("wp", [P, CT, C])
        xwq = sb("xwq", [P, CT, C])
        xwk = sb("xwk", [P, CT, C])
        xwv = sb("xwv", [P, CT, C])
        xwo = sb("xwo", [P, CT, C])
        bpS = sb("bpS", [P, C])
        b2S = sb("b2S", [E, C])
        b1S = sb("b1S", [P, E * FT])
        b1E = sb("b1E", [P, 2, FT])
        rS = sb("rS", [P, CT, E])
        idf = sb("idf", [P, P])
        idb = sb("idb", [P, P], BF16)
        dS = sb("dS", [P, P], BF16)
        dTS = sb("dTS", [P, P], BF16)
        selS = sb("selS", [P, D + 1])
        slB = sb("slB", [P, H])
        sl8 = sb("sl8", [P, H])
        slP = sb("slP", [P, PARTS, H], BF16)
        slPF = sb("slPF", [P, PARTS, H])
        slR = sb("slR", [P, H])
        slopeDiag = sb("slopeDiag", [P, 2, PARTS, P], BF16)
        slRow = sb("slRow", [6 * H, 8])
        slRowB = sb("slRowB", [6 * H, 4], BF16)
        mU8 = sb("mU8", [1, NX], U8)
        mRow = sb("mRow", [1, NXP], BF16)
        CM = sb("CM", [P, TT, 4])
        NM = sb("NM", [P, TT])
        NR = sb("NR", [P, TT])
        SHW = sb("SHW", [P, P], BF16)
        SH = SHW[:, 0:PARTS * TT].rearrange("p (s t) -> p s t", t=TT)
        MT = sb("MT", [PARTS * TT, P], BF16)
        RC = sb("RC", [P, 2, 4, 1])
        ATT = sb("ATT", [P, 2, CT, P])
        stats = sb("stats", [P, 2, 6])
        agg = sb("agg", [P, 2, 2])
        var = sb("var", [P, 2, 5])
        L = sb("L", [P, TT, E])
        G = sb("G", [P, TT, E])
        rank = sb("rank", [P, TT, E])
        cmp_ = sb("cmp_", [P, TT, E])
        beat = sb("beat", [P, TT, E])
        top = sb("top", [P, TT, 1])
        pickS = sb("pickS", [6 * H, PARTS])
        GT = PT[0:E, 0:4, :].rearrange("p a b -> p (a b)")

        B = [ps(f"B{i}", [P, QB]) for i in range(8)]
        S = B[0:SBANKS]
        R = B[SBANKS:SBANKS + RBANKS]
        O = B[6:8]

        qD = nc.dram_tensor("qD", [PARTS, C, N], BF16).ap()
        kD = nc.dram_tensor("kD", [PARTS, C, N], BF16).ap()
        qxD = nc.dram_tensor("qxD", [PARTS, C, N], BF16).ap()
        kxD = nc.dram_tensor("kxD", [PARTS, C, NXP], BF16).ap()
        slD = nc.dram_tensor("slD", [6 * H, N], BF16).ap()
        sdD = nc.dram_tensor("sdD", [H * P, PARTS * P], BF16).ap()

        s_w = sem("weights_loaded")
        s_x = sem("stream_loaded")
        s_c = sem("context_loaded")
        s_k = sem("constants_loaded")
        s_rope = sem("rope_tables_loaded")
        s_m = sem("misc_constants_loaded")
        s_zero = sem("buffers_cleared")
        s_prep = sem("proj_ready")
        s_prepfree = sem("proj_read")
        s_chain = sem("prep_chain")
        s_q = sem("prep_value_ready")
        s_hi = sem("prep_high_ready")
        s_r = sem("prep_rest_ready")
        s_mi = sem("prep_middle_ready")
        s_lo = sem("prep_parts_ready")
        s_st = [sem(f"parts_stored{i}") for i in range(3)]
        s_v = sem("v_proj_ready")
        s_vs = sem("v_proj_saved")
        s_sl = sem("slope_chain")
        s_slout = sem("slope_rows_stored")
        s_sdr = sem("slope_diag_ready")
        s_sdo = [sem(f"slope_diag_stored{i}") for i in range(2)]
        s_mask = sem("mask_row_ready")
        s_mrow = sem("mask_row_placed")
        s_const = sem("constant_rows_placed")
        s_tr = sem("attention_transposed")
        s_att = sem("attention_transpose_saved")
        s_pj = sem("output_projected")
        s_ln = sem("norm_chain")
        s_var = sem("variance_ready")
        s_sd = sem("deviation_ready")
        s_xn = sem("stream_normed")
        s_xt = sem("stream_transposed")
        s_xts = sem("stream_transpose_saved")
        s_log = sem("logits_ready")
        s_gl = sem("logits_saved")
        s_gc = sem("gate_chain")
        s_ge = sem("gate_exp")
        s_g = sem("gates_ready")
        s_gt = sem("gates_transposed")
        s_gts = sem("gates_transpose_saved")
        s_b2 = sem("bias_mix_ready")
        s_acc0 = sem("experts_sum_started")
        s_w1 = [sem(f"w1_loaded{i}") for i in range(2)]
        s_w2 = [sem(f"w2_loaded{i}") for i in range(2)]
        s_hid = sem("hidden_ready")
        s_gelu = sem("gelu_done")
        s_b1 = sem("expert_bias_ready")
        s_moe = sem("expert_ready")
        s_moef = sem("expert_added")
        s_out = sem("output_stored")

        class Att:
            def __init__(self, name):
                self.loaded = [sem(f"{name}_operands_loaded{i}") for i in range(RING)]
                self.shift_loaded = sem(f"{name}_shift_loaded")
                self.scores = sem(f"{name}_scores_ready")
                self.exps = sem(f"{name}_exps_done")
                self.pv = sem(f"{name}_pv_done")
                self.saved = sem(f"{name}_acc_saved")
                self.filled = sem(f"{name}_ring_filled")
                self.freed = sem(f"{name}_ring_freed")
                self.sums = sem(f"{name}_sums_taken")
                self.v = sem(f"{name}_v_staged")
                self.chain = sem(f"{name}_shift_chain")
                self.cols = sem(f"{name}_shift_cols_ready")
        SA, XA = Att("self"), Att("cross")

        block = ctx.enter_context(nc.Block())

        def items_of(kind, n):
            return [(kind, half, c * n, n) for half in range(CT) for c in range(4)]
        PREP1 = items_of("q", QB) + items_of("k", QB) + items_of("xk", NXP // 4)
        PREP2 = items_of("xq", QB)
        dest = {"q": qD, "k": kD, "xk": kxD, "xq": qxD}
        NPREP = len(PREP1)

        def head_steps(engine, body):
            body(0, 0, 0)
            with engine.Fori(0, HEADS_LOOPED // RING) as it:
                for c in range(RING):
                    h = it * RING + (1 + c)
                    body(h, (1 + c) % RING, it + (1 + c) // RING)
            for h in range(HEADS_LOOPED + 1, H):
                body(h, h % RING, h // RING)

        @block.sync
        def _(sp):
            sp.dma_start(XT[:, :, :], xT.rearrange("(k p) n -> p k n", p=P)).then_inc(s_x, 16)
            sp.dma_start(wqkv[:, :, :], wqkvT.rearrange("(k p) n -> p k n", p=P)).then_inc(s_w, 16)
            sp.dma_start(wrot[:, :, :], wrotT.rearrange("(k p) n -> p k n", p=P)).then_inc(s_w, 16)
            sp.dma_start(cosS, cosT).then_inc(s_rope, 16)
            sp.dma_start(sinS, sinT).then_inc(s_rope, 16)
            sp.dma_start(CX[:, :, 0:NX], ctxT.rearrange("(k p) n -> p k n", p=P)).then_inc(s_c, 16)
            for w, src in ((xwk, xwkT), (xwv, xwvT), (xwq, xwqT), (wp, wpT), (xwo, xwoT)):
                sp.dma_start(w[:, :, :], src.rearrange("(k p) n -> p k n", p=P)).then_inc(s_c, 16)
            sp.dma_start(X[:, :, :], x.rearrange("(t p) c -> p t c", p=P)).then_inc(s_m, 16)
            sp.dma_start(bpS[:, :], bp.partition_broadcast(P)).then_inc(s_m, 16)
            sp.dma_start(b2S[:, :], b2).then_inc(s_m, 16)
            sp.dma_start(b1S[:, :], b1T).then_inc(s_m, 16)
            sp.dma_start(rS[:, :, :], rT.rearrange("(k p) n -> p k n", p=P)).then_inc(s_m, 16)
            for r in range(RING):
                sp.dma_start(QO[0:S0, r, :], constQ).then_inc(s_const, 16)
                sp.dma_start(KO[0:S0, r, 0, :], constKL).then_inc(s_const, 16)
                sp.dma_start(KO[0:S0, r, 1, :], constK0).then_inc(s_const, 16)
                for v in range(2):
                    sp.dma_start(KO[A_ROWS:B_ROWS, r, v, :], ones3).then_inc(s_const, 16)

            def store_parts(items, first):
                for n, (kind, half, c0, w) in enumerate(items):
                    i = first + n
                    sp.wait_ge(s_lo, i + 1)
                    sp.dma_start(dest[kind][:, half * P:(half + 1) * P, c0:c0 + w].rearrange("s r c -> r s c"),
                                 parts[:, i % 3, :, 0:w]).then_inc(s_st[i % 3], 16)

            sp.wait_ge(s_sl, 1)
            sp.dma_start(slD, slopeF).then_inc(s_slout, 16)
            for h in range(H):
                sp.wait_ge(s_sdr, h + 1)
                sp.dma_start(sdD[h * P:(h + 1) * P, :], slopeDiag[:, h % 2, :, :].rearrange("p s j -> p (s j)")).then_inc(s_sdo[h % 2], 16)
            store_parts(PREP1, 0)
            for i in range(3):
                sp.wait_ge(s_st[i], 16 * (NPREP // 3))
            sp.wait_ge(s_slout, 16)
            sp.wait_ge(s_sdo[0], 16 * H // 2)
            sp.wait_ge(s_sdo[1], 16 * H // 2)
            sp.wait_ge(s_const, 16 * 5 * RING)

            def attention_loads(A, plan, qsrc, ksrc):
                alibi = A is SA

                def load(h, c):
                    rows = bass.ds(h * D, D)
                    q = QO[S0:A_ROWS, c, :]
                    ld = A.loaded[c]
                    sp.dma_start(q[0:3 * D, :], qsrc[0:3, rows, :]).then_inc(ld, 16)
                    sp.dma_start(q[3 * D:5 * D, :], qsrc[0:2, rows, :]).then_inc(ld, 16)
                    sp.dma_start(q[5 * D:6 * D, :], qsrc[0, rows, :]).then_inc(ld, 16)
                    for v in range(2 if alibi else 1):
                        k = KO[S0:A_ROWS, c, v, 0:plan.keys]
                        row = 0
                        for part, times in ((0, 3), (1, 2), (2, 1)):
                            sp.dma_start(k[row:row + times * D, :],
                                         ksrc[part:part + 1, rows, :].to_broadcast([times, D, plan.keys])).then_inc(ld, 16)
                            row += times * D
                    if alibi:
                        srows = bass.ds(h * 6, 6)
                        sp.dma_start(QO[0:BIAS_ROWS:2, c, :], slD[srows, :]).then_inc(ld, 16)
                        sp.dma_start(KO[1:BIAS_ROWS:2, c, 0, :], slD[srows, :]).then_inc(ld, 16)
                        sp.dma_start(SD[:, c, :, :].rearrange("p s j -> p (s j)"), sdD[bass.ds(h * P, P), :]).then_inc(ld, 16)

                def place_shift(h, c):
                    sp.wait_ge(A.freed, plan.shift_end(h))
                    for s in range(PARTS):
                        sp.dma_start(QO[A_ROWS + s:A_ROWS + s + 1, c, :],
                                     MT[s * TT:(s + 1) * TT, :]).then_inc(A.shift_loaded, 16)

                for h in range(RING):
                    load(h, h)
                place_shift(0, 0)

                def step(h, c, turn):
                    whole = isinstance(h, int)
                    if not (whole and (h == 0 or h + 2 >= H)):
                        sp.wait_ge(A.scores, plan.nu * h)
                        load(h + 2, (c + 2) % RING)
                    if not (whole and h + 1 >= H):
                        place_shift(h + 1, (c + 1) % RING)
                head_steps(sp, step)

            attention_loads(SA, SELF, qD, kD)
            sp.wait_ge(SA.scores, SELF.nu * H)
            for r in range(RING):
                sp.dma_start(QO[0:S0, r, :], constQX).then_inc(s_mrow, 16)
                sp.dma_start(KO[0:BIAS_ROWS, r, 0, :], constK0[0:BIAS_ROWS, :]).then_inc(s_mrow, 16)
                if r == 0:
                    sp.wait_ge(s_mask, 2)
                sp.dma_start(KO[MASK_ROW:MASK_ROW + 1, r, 0, 0:NXP], mRow[:, :]).then_inc(s_mrow, 16)
            store_parts(PREP2, NPREP)
            for i in range(3):
                sp.wait_ge(s_st[i], 16 * ((NPREP + len(PREP2) - i + 2) // 3))
            attention_loads(XA, CROSS, qxD, kxD)

            def load_w1(e, b):
                sp.dma_start(W1[:, b, :, :], w1T[bass.ds(e * C, C), :].rearrange("(k p) f -> p k f", p=P)).then_inc(s_w1[b], 16)

            def load_w2(e, b):
                sp.dma_start(W2[:, b, :, :], w2T[bass.ds(e * F, F), :].rearrange("(f p) c -> p f c", p=P)).then_inc(s_w2[b], 16)
            sp.wait_ge(XA.scores, CROSS.nu * H)
            for e in range(2):
                load_w1(e, e)
                load_w2(e, e)
            with sp.Fori(0, E // 2 - 1) as it:
                for b in range(2):
                    e = it * 2 + b
                    sp.wait_ge(s_hid, e * (4 * FT) + 4 * FT)
                    load_w1(e + 2, b)
                    sp.wait_ge(s_moe, e * TT + TT + 8)
                    load_w2(e + 2, b)
            for t in range(TT):
                sp.wait_ge(s_xn, 2 * TT + t + 1)
                sp.dma_start(out[t * P:(t + 1) * P, :], X[:, t, :]).then_inc(s_out, 16)
            sp.wait_ge(s_out, 16 * TT)

        @block.gpsimd
        def _(pool):
            pool.dma_start(slB[:, :], slopes.partition_broadcast(P)).then_inc(s_k, 16)
            pool.dma_start(slRow[:, 0:1],
                           slopes.rearrange("(h s o) -> h s o", s=1, o=1).to_broadcast([H, 6, 1])).then_inc(s_k, 16)
            pool.dma_start(mU8[:, :], mask).then_inc(s_k, 16)
            for dst, src in ((idf, ident), (idb, identb), (dS, dist), (dTS, distT), (selS, sel), (pickS, pick)):
                pool.dma_start(dst[:, :], src).then_inc(s_k, 16)
            pool.memset(CX[:, :, NX:NXP], 0.0).then_inc(s_zero, 1)
            pool.memset(VS[:, :, :, D:2 * D], 0.0).then_inc(s_zero, 1)
            pool.wait_ge(s_zero, 2)
            pool.memset(VS[:, :, :, D:D + 1], 1.0).then_inc(s_zero, 1)

            def stage(A, plan, V):
                nk = plan.nk

                def step(h, c, turn):
                    if not (isinstance(h, int) and h < RING):
                        pool.wait_ge(A.pv, plan.nb * (h - RING + 1))
                    pool.tensor_copy(VS[:, c, 0:nk, 0:D], V[:, 0:nk, bass.ds(h * D, D)]).then_inc(A.v, 1)
                step(0, 0, 0)
                step(1, 1, 0)
                step(2, 2, 0)
                with pool.Fori(1, H // RING) as it:
                    for c in range(RING):
                        step(it * RING + c, c, it)
                for h in range(H // RING * RING, H):
                    step(h, h % RING, h // RING)
            pool.wait_ge(s_vs, TT)
            stage(SA, SELF, VA)
            pool.wait_ge(s_vs, TT + NXP // P)
            pool.wait_ge(SA.pv, SELF.nb * H)
            stage(XA, CROSS, VX)

        @block.tensor
        def _(pe):
            def prep(items, first):
                for n, (kind, half, c0, w) in enumerate(items):
                    i = first + n
                    wt, off = {"q": (wqkv, 0), "k": (wqkv, C), "xk": (xwk, 0), "xq": (xwq, 0)}[kind]
                    src = CX if kind == "xk" else XT
                    if i >= 2:
                        pe.wait_ge(s_prepfree, i - 1)
                    for k in range(CT):
                        mm = pe.matmul(B[2 * (i % 2)][:, 0:w], wt[:, k, off + half * P:off + (half + 1) * P],
                                       src[:, k, c0:c0 + w], start=(k == 0), stop=(k == CT - 1))
                    if kind in "qk":
                        for k in range(CT):
                            mm = pe.matmul(B[2 * (i % 2) + 1][:, 0:w], wrot[:, k, off + half * P:off + (half + 1) * P],
                                           src[:, k, c0:c0 + w], start=(k == 0), stop=(k == CT - 1))
                    mm.then_inc(s_prep, 1)

            def v_proj(src, wt, off, n, first):
                for t in range(n):
                    i = first + t
                    if i >= 2:
                        pe.wait_ge(s_vs, i - 1)
                    for k in range(CT):
                        mm = pe.matmul(B[4 + i % 2][:, 0:C], src[:, k, t * P:(t + 1) * P], wt[:, k, off:off + C],
                                       start=(k == 0), stop=(k == CT - 1))
                    mm.then_inc(s_v, 1)

            pe.wait_ge(s_x, 16)
            pe.wait_ge(s_w, 32)
            prep(PREP1[0:16], 0)
            v_proj(XT, wqkv, 2 * C, TT, 0)
            pe.wait_ge(s_c, 16 * 6)
            pe.wait_ge(s_zero, 3)
            prep(PREP1[16:], 16)
            v_proj(CX, xwv, 0, NXP // P, TT)

            def attention(A, plan):
                alibi = A is SA
                nk, ch = plan.nk, plan.chunk

                def ring_item(item, pos, bank, h, c):
                    kind, a, b, ahead = item
                    if not isinstance(pos, int) or pos + width(item) > RBANKS:
                        pe.wait_ge(A.freed, pos + (width(item) - RBANKS))
                    slot = R[bank % RBANKS]
                    if kind == "max":
                        t, k0, k1 = a, b * ch, (b + 1) * ch
                        c2 = (c + ahead) % RING
                        if a == 0 and b == 0:
                            pe.wait_ge(A.loaded[c2], loads_due(h, c, ahead))
                        q = QO[0:A_ROWS, c2, t * P:(t + 1) * P]
                        low = min(max(t * P, k0), k1) - k0 if alibi else ch
                        diag = alibi and k0 <= t * P < k1
                        if low:
                            mm = pe.matmul(slot[:, 0:low], q, KO[0:A_ROWS, c2, 0, k0:k0 + low],
                                           start=True, stop=True, skip_group_check=True)
                        if low < ch:
                            mm = pe.matmul(slot[:, low:ch], q, KO[0:A_ROWS, c2, 1, k0 + low:k1],
                                           start=(low == 0), stop=not diag, skip_group_check=True)
                        if diag:
                            for s in range(PARTS):
                                mm = pe.matmul(slot[:, low:low + P], SD[:, c2, s, :], dS[:, :],
                                               start=False, stop=(s == PARTS - 1), skip_group_check=True)
                        mm.then_inc(A.filled, 1)
                    elif kind == "shift":
                        pe.wait_ge(A.cols, h + 2)
                        pe.transpose(slot[:, 0:P // 2].bitcast(BF16), SHW[:, :],
                                     idb[:, :]).then_inc(A.filled, 1)
                    else:
                        pe.wait_ge(A.saved, (h + ahead) * NQB + (a + 1))
                        for t in range(4):
                            mm = pe.matmul(slot[:, t * 32:t * 32 + D + 1], OS[:, a % 2, t * P:(t + 1) * P], selS[:, :],
                                           start=True, stop=True, skip_group_check=True)
                        mm.then_inc(A.filled, 1)

                turn_now = [0]

                def loads_due(h, c, ahead):
                    per = 16 * (12 if alibi else 6)
                    if isinstance(h, int):
                        return per * ((h + ahead) // RING + 1)
                    return (turn_now[0] + ((c + ahead) // RING + 1)) * per

                def scores_unit(u, h, c):
                    qb, kt = u // nk, u % nk
                    if not (isinstance(h, int) and h == 0 and u < SBANKS):
                        pe.wait_ge(A.exps, plan.nu * h + (u + 1 - SBANKS))
                    bank = S[(c * plan.nu + u) % SBANKS]
                    q0 = qb * QB
                    lo = min(max(kt * P - q0, 0), QB) if alibi else 0
                    diag = alibi and q0 <= kt * P < q0 + QB
                    up = lo + P if diag else lo
                    stat = [KO[0:B_ROWS, c, v, kt * P:(kt + 1) * P] for v in range(2)]
                    if up:
                        mm = pe.matmul(bank[:, 0:up], stat[1], QO[0:B_ROWS, c, q0:q0 + up],
                                       start=True, stop=not diag, skip_group_check=True)
                    if diag:
                        for s in range(PARTS):
                            mm = pe.matmul(bank[:, lo:up], SD[:, c, s, :], dTS[:, :],
                                           start=False, stop=(s == PARTS - 1), skip_group_check=True)
                    if up < QB:
                        mm = pe.matmul(bank[:, up:QB], stat[0], QO[0:B_ROWS, c, q0 + up:q0 + QB],
                                       start=(up == 0), stop=True, skip_group_check=True)
                    mm.then_inc(A.scores, 1)

                def pv_batch(b, h, c):
                    pe.wait_ge(A.exps, plan.nu * h + (4 * b + 4))
                    for u in range(4 * b, 4 * b + 4):
                        qb, kt = u // nk, u % nk
                        if kt == 0 and not (isinstance(h, int) and h == 0 and qb < 2):
                            pe.wait_ge(A.saved, h * NQB + (qb - 1))
                        g = u % 4
                        mm = pe.matmul(O[qb % 2][32 * g:32 * g + 32, :], VS[:, c, kt, :],
                                       PT[:, (c * plan.nu + u) % PRING, :],
                                       start=(kt < 4), stop=(kt + 4 >= nk), skip_group_check=True)
                    mm.then_inc(A.pv, 1)

                def step(h, c, turn):
                    whole = isinstance(h, int)
                    first = whole and h == 0
                    turn_now[0] = turn
                    pos = plan.ring_before(h)
                    static = plan.static_before(h, c)
                    pe.wait_ge(A.shift_loaded, (h + 1) * 16 * PARTS)
                    off = 0

                    def ring(items):
                        nonlocal off
                        for item in items:
                            ring_item(item, pos + off, static + off, h, c)
                            off += width(item)
                    for b in range(plan.nb):
                        items = plan.ring_items(b, h)
                        cuts = [len(items) * n // 4 for n in range(5)]
                        for n in range(4):
                            scores_unit(4 * b + n, h, c)
                            ring(items[cuts[n]:cuts[n + 1]])
                            if n == 1 and b > 0:
                                pv_batch(b - 1, h, c)
                            elif n == 1:
                                if not first:
                                    pv_batch(plan.nb - 1, h - 1, (c - 1) % RING)
                                pe.wait_ge(A.v, h + 1)

                pos = 0
                for item in plan.prologue:
                    ring_item(item, pos, pos, -1, RING - 1)
                    pos += width(item)
                head_steps(pe, step)
                pv_batch(plan.nb - 1, H - 1, (H - 1) % RING)
                end = plan.ring_before(H)
                for q in range(NQB):
                    if plan.last_batch[q] + 3 >= plan.nb:
                        ring_item(("sum", q, 0, 0), end, end, H - 1, 0)
                        end += 1

            def project_norm(call, A, plan, w):
                pe.wait_ge(A.freed, plan.ring_before(H) + 1)
                b0 = call * TT
                for s in range(TT + 3):
                    if s < TT:
                        if s >= 2:
                            pe.wait_ge(s_att, b0 + s - 1)
                        for k in range(CT):
                            mm = pe.transpose(B[s % 2][:, k * P:(k + 1) * P], AT[:, s, k * P:(k + 1) * P], idf[:, :])
                        mm.then_inc(s_tr, 1)
                    t = s - 1
                    if 0 <= t < TT:
                        pe.wait_ge(s_att, b0 + t + 1)
                        if t >= 2:
                            pe.wait_ge(s_xn, b0 + t - 1)
                        for k in range(CT):
                            mm = pe.matmul(B[2 + t % 2][:, 0:C], ATT[:, t % 2, k, :], w[:, k, :],
                                           start=(k == 0), stop=(k == CT - 1))
                        mm.then_inc(s_pj, 1)
                    t = s - 3
                    if 0 <= t < TT:
                        pe.wait_ge(s_xn, b0 + t + 1)
                        if t >= 2:
                            pe.wait_ge(s_xts, b0 + t - 1)
                        for k in range(CT):
                            mm = pe.transpose(O[t % 2][:, k * P:(k + 1) * P], X[:, t, k * P:(k + 1) * P], idf[:, :])
                        mm.then_inc(s_xt, 1)

            pe.wait_ge(s_prepfree, NPREP)
            pe.wait_ge(s_vs, TT + NXP // P)
            pe.wait_ge(s_k, 16 * 9)
            pe.wait_ge(s_const, 16 * 5 * RING)
            attention(SA, SELF)
            project_norm(0, SA, SELF, wp)
            pe.wait_ge(s_xts, TT)
            pe.wait_ge(s_xn, TT)
            prep(PREP2, NPREP)
            pe.wait_ge(s_prepfree, NPREP + len(PREP2))
            pe.wait_ge(s_mrow, 16 * 3 * RING)
            attention(XA, CROSS)
            project_norm(1, XA, CROSS, xwo)

            pe.wait_ge(s_xts, 2 * TT)
            for t in range(TT):
                for k in range(CT):
                    mm = pe.matmul(B[4][:, t * E:(t + 1) * E], XT[:, k, t * P:(t + 1) * P], rS[:, k, :],
                                   start=(k == 0), stop=(k == CT - 1), skip_group_check=True)
            mm.then_inc(s_log, 1)
            pe.wait_ge(s_g, 1)
            for t in range(TT):
                mm = pe.transpose(B[t // 4][0:E, (t % 4) * P:(t % 4 + 1) * P], G[:, t, :], idf[:, :])
            mm.then_inc(s_gt, 1)
            pe.wait_ge(s_gts, 4)
            for t in range(TT):
                if t >= 2:
                    pe.wait_ge(s_acc0, t - 1)
                pe.matmul(O[t % 2][:, 0:C], GT[:, t * P:(t + 1) * P], b2S[:, :], start=True, stop=True).then_inc(s_b2, 1)
            pe.wait_ge(s_acc0, TT)

            HB = B[0:4]
            OB = B[4:8]
            pe.sem_inc(s_gelu, 4)
            pe.sem_inc(s_moe, 8)
            pe.sem_inc(s_moef, 4)

            def first_layer(e, b, tb):
                for f in range(FT):
                    n = tb * FT + f
                    pe.wait_ge(s_gelu, e * (4 * FT) + n + 1)
                    for k in range(CT):
                        mm = pe.matmul(HB[f % 4][:, :], W1[:, b, k, f * P:(f + 1) * P], XT[:, k, tb * QB:(tb + 1) * QB],
                                       start=(k == 0), stop=(k == CT - 1))
                    mm.then_inc(s_hid, 1)

            def second_layer(e, b, tb):
                pe.wait_ge(s_gelu, e * (4 * FT) + (tb + 1) * FT + 4)
                for j in range(4):
                    pe.wait_ge(s_moef, e * TT + tb * 4 + j + 1)
                    for f in range(FT):
                        mm = pe.matmul(OB[j][:, 0:C], HID[:, tb % 2, f, j * P:(j + 1) * P], W2[:, b, f, :],
                                       start=(f == 0), stop=(f == FT - 1))
                    mm.then_inc(s_moe, 1)

            with pe.Fori(0, E // 2) as it:
                for b in range(2):
                    e = it * 2 + b
                    pe.wait_ge(s_w1[b], it * 16 + 16)
                    first_layer(e, b, 0)
                    pe.wait_ge(s_w2[b], it * 16 + 16)
                    for tb in range(1, 4):
                        first_layer(e, b, tb)
                        second_layer(e, b, tb - 1)
                    second_layer(e, b, 3)

        @block.scalar
        def _(act):
            def prep(items, first):
                n = len(items)
                for s in range(n + 1):
                    if s < n:
                        i, w = first + s, items[s][3]
                        act.wait_ge(s_q, i + 1)
                        if i >= 3:
                            act.wait_ge(s_st[i % 3], 16 * (i // 3))
                        act.activation(parts[:, i % 3, 0, 0:w], QF[:, i % 3, 0:w], ACT.Copy).then_inc(s_hi, 1)
                    if s >= 1:
                        i, w = first + s - 1, items[s - 1][3]
                        act.wait_ge(s_r, i + 1)
                        act.activation(parts[:, i % 3, 1, 0:w], RF[:, i % 2, 0:w], ACT.Copy).then_inc(s_mi, 1)

            def v_save(V, n, first):
                for t in range(n):
                    i = first + t
                    act.wait_ge(s_v, i + 1)
                    act.activation(V[:, t, :], B[4 + i % 2][:, 0:C], ACT.Copy).then_inc(s_vs, 1)

            prep(PREP1[0:16], 0)
            v_save(VA, TT, 0)
            prep(PREP1[16:], 16)
            v_save(VX, NXP // P, TT)

            def attention(A, plan):
                def save(q, h):
                    act.wait_ge(A.pv, plan.nb * h + (plan.last_batch[q] + 1))
                    if not (isinstance(h, int) and h == 0 and q < 2):
                        act.wait_ge(A.sums, h * NQB + (q - 1))
                    act.activation(OS[:, q % 2, :], O[q % 2][:, :], ACT.Copy).then_inc(A.saved, 1)

                def step(h, c, turn):
                    first = isinstance(h, int) and h == 0
                    for b in range(plan.nb):
                        for u in range(4 * b, 4 * b + 4):
                            act.wait_ge(A.scores, plan.nu * h + (u + 1))
                            if u % 4 == 0 and not (first and u < PRING):
                                act.wait_ge(A.pv, plan.nb * h + (b - PRING // 4 + 1))
                            act.activation(PT[:, (c * plan.nu + u) % PRING, :], S[(c * plan.nu + u) % SBANKS][:, :],
                                           ACT.Exp).then_inc(A.exps, 1)
                            if u % 4 == 1:
                                for q, back in plan.saves(b, first):
                                    save(q, h + back)
                head_steps(act, step)
                for q in range(NQB):
                    if plan.last_batch[q] + 2 >= plan.nb:
                        save(q, H - 1)

            def root(i):
                act.wait_ge(s_var, i + 1)
                act.activation(var[:, i % 2, 1:2], var[:, i % 2, 0:1], ACT.Sqrt).then_inc(s_sd, 1)

            def transposes(call):
                b0 = call * TT
                for s in range(TT + 3):
                    if s < TT:
                        act.wait_ge(s_tr, b0 + s + 1)
                        if s >= 2:
                            act.wait_ge(s_pj, b0 + s - 1)
                        act.activation(ATT[:, s % 2, :, :].rearrange("p k j -> p (k j)"), B[s % 2][:, 0:C],
                                       ACT.Copy).then_inc(s_att, 1)
                    if 1 <= s <= TT:
                        root(b0 + s - 1)
                    t = s - 3
                    if t >= 0:
                        act.wait_ge(s_xt, b0 + t + 1)
                        act.activation(XT[:, :, t * P:(t + 1) * P], O[t % 2][:, 0:C].rearrange("p (k j) -> p k j", k=CT),
                                       ACT.Copy).then_inc(s_xts, 1)

            attention(SA, SELF)
            transposes(0)
            prep(PREP2, NPREP)
            attention(XA, CROSS)
            transposes(1)
            act.wait_ge(s_gc, 2)
            act.activation(G[:, :, :], cmp_[:, :, :], ACT.Exp).then_inc(s_ge, 1)
            act.wait_ge(s_gt, 1)
            for j in range(4):
                act.activation(GT[:, j * QB:(j + 1) * QB], B[j][0:E, :], ACT.Copy).then_inc(s_gts, 1)
            HB = B[0:4]
            with act.Fori(0, E // 2) as it:
                for b in range(2):
                    e = it * 2 + b
                    act.activation(b1E[:, b, :], b1S[:, bass.ds(e * FT, FT)], ACT.Copy).then_inc(s_b1, 1)
                    act.wait_ge(s_b1, e + 1)
                    for tb in range(4):
                        act.wait_ge(s_moe, e * TT + tb * 4 + 4)
                        for f in range(FT):
                            act.wait_ge(s_hid, e * (4 * FT) + tb * FT + f + 1)
                            act.activation(HID[:, tb % 2, f, :], HB[f % 4][:, :], ACT.Gelu,
                                           bias=b1E[:, b, f:f + 1]).then_inc(s_gelu, 1)
            for t in range(TT):
                root(2 * TT + t)

        @block.vector
        def _(dve):
            links = {}

            def link(ins, s):
                links[s] = links.get(s, 0) + 1
                ins.then_inc(s, 1)
                dve.wait_ge(s, links[s])

            dve.wait_ge(s_k, 16 * 9)
            link(dve.memset(slopeF, 1.0), s_chain)
            link(dve.memset(SHW[:, :], 0.0), s_chain)
            link(dve.tensor_scalar(slRow[:, 1:2], slRow[:, 0:1], MAX_BIAS, None, ALU.mult), s_chain)
            link(dve.tensor_copy(slRowB[:, 0:1], slRow[:, 1:2]), s_chain)
            link(dve.tensor_tensor(slRow[:, 2:3], slRow[:, 1:2], slRowB[:, 0:1], ALU.subtract), s_chain)
            link(dve.tensor_copy(slRowB[:, 1:2], slRow[:, 2:3]), s_chain)
            link(dve.tensor_tensor(slRowB[:, 2:3], slRow[:, 2:3], slRowB[:, 1:2], ALU.subtract), s_chain)
            link(dve.tensor_tensor(slRow[:, 3:6], slRowB[:, 0:3], pickS[:, :], ALU.mult), s_chain)
            link(dve.tensor_reduce(slRow[:, 6:7], slRow[:, 3:6], AX.X, ALU.add), s_chain)
            dve.tensor_scalar(slopeF, slopeF, slRow[:, 6:7], None, ALU.mult).then_inc(s_sl, 1)
            link(dve.tensor_scalar(sl8[:, :], slB[:, :], MAX_BIAS, None, ALU.mult), s_chain)
            link(dve.tensor_copy(slP[:, 0, :], sl8[:, :]), s_chain)
            link(dve.tensor_tensor(slR[:, :], sl8[:, :], slP[:, 0, :], ALU.subtract), s_chain)
            link(dve.tensor_copy(slP[:, 1, :], slR[:, :]), s_chain)
            link(dve.tensor_tensor(slP[:, 2, :], slR[:, :], slP[:, 1, :], ALU.subtract), s_chain)
            link(dve.tensor_copy(slPF[:, :, :], slP[:, :, :]), s_chain)
            for h in range(H):
                if h >= 2:
                    dve.wait_ge(s_sdo[h % 2], 16 * (h // 2))
                for s in range(PARTS):
                    ins = dve.tensor_scalar(slopeDiag[:, h % 2, s, :], idf[:, :], slPF[:, s, h:h + 1], None, ALU.mult)
                ins.then_inc(s_sdr, 1)
            link(dve.memset(mRow[:, :], MASKED), s_mask)
            dve.tensor_scalar(mRow[:, 0:NX], mU8[:, :], -1.0, -MASKED, ALU.add, ALU.mult).then_inc(s_mask, 1)
            dve.wait_ge(s_m, 16 * 5)
            link(dve.tensor_tensor(X[:, :, :], X[:, :, :], bpS[:, :].unsqueeze(1).to_broadcast([P, TT, C]), ALU.add), s_chain)

            def prep(items, first):
                n = len(items)
                for s in range(n + 2):
                    if s < n:
                        i = first + s
                        kind, half, c0, w = items[s]
                        dve.wait_ge(s_prep, i + 1)
                        if i >= 3:
                            dve.wait_ge(s_r, i - 2)
                        if kind in "qk":
                            if i >= 2:
                                dve.wait_ge(s_q, i - 1)
                            dve.tensor_tensor(T1[:, i % 2, 0:w], B[2 * (i % 2)][:, 0:w], cosS[:, c0:c0 + w], ALU.mult)
                            ins = dve.tensor_tensor(T2[:, i % 2, 0:w], B[2 * (i % 2) + 1][:, 0:w], sinS[:, c0:c0 + w], ALU.mult)
                            ins.then_inc(s_prepfree, 1)
                            dve.wait_ge(s_prepfree, i + 1)
                            dve.tensor_tensor(QF[:, i % 3, 0:w], T1[:, i % 2, 0:w], T2[:, i % 2, 0:w], ALU.add).then_inc(s_q, 1)
                        else:
                            dve.tensor_scalar(QF[:, i % 3, 0:w], B[2 * (i % 2)][:, 0:w], SCALE if kind == "xq" else 1.0, None,
                                              ALU.mult).then_inc(s_prepfree, 1)
                            dve.wait_ge(s_prepfree, i + 1)
                            dve.sem_inc(s_q, 1)
                    if 1 <= s <= n:
                        i, w = first + s - 1, items[s - 1][3]
                        dve.wait_ge(s_hi, i + 1)
                        if i >= 2:
                            dve.wait_ge(s_lo, i - 1)
                        dve.tensor_tensor(RF[:, i % 2, 0:w], QF[:, i % 3, 0:w], parts[:, i % 3, 0, 0:w], ALU.subtract).then_inc(s_r, 1)
                    if s >= 2:
                        i, w = first + s - 2, items[s - 2][3]
                        dve.wait_ge(s_mi, i + 1)
                        dve.tensor_tensor(parts[:, i % 3, 2, 0:w], RF[:, i % 2, 0:w], parts[:, i % 3, 1, 0:w], ALU.subtract).then_inc(s_lo, 1)

            dve.wait_ge(s_rope, 32)
            prep(PREP1[0:16], 0)
            prep(PREP1[16:], 16)

            def attention(A, plan):
                ch = plan.chunk

                def ring_item(item, pos, bank, h):
                    kind, a, b, ahead = item
                    slot = R[bank % RBANKS]
                    if kind == "max":
                        dve.wait_ge(A.filled, pos + 1)
                        dve.tensor_reduce(CM[:, a, b:b + 1], slot[:, 0:ch], AX.X, ALU.max).then_inc(A.freed, 1)
                        if (a, b) == (TT - 1, 3):
                            n = (h + ahead) * 4
                            dve.wait_ge(A.freed, pos + 1)
                            dve.tensor_reduce(NM[:, :], CM[:, :, :], AX.X, ALU.max, negate=True).then_inc(A.chain, 1)
                            dve.wait_ge(A.chain, n + 1)
                            dve.tensor_copy(SH[:, 0, :], NM[:, :]).then_inc(A.chain, 1)
                            dve.wait_ge(A.chain, n + 2)
                            dve.tensor_tensor(NR[:, :], NM[:, :], SH[:, 0, :], ALU.subtract).then_inc(A.chain, 1)
                            dve.wait_ge(A.chain, n + 3)
                            dve.tensor_copy(SH[:, 1, :], NR[:, :]).then_inc(A.chain, 1)
                            dve.wait_ge(A.chain, n + 4)
                            dve.tensor_tensor(SH[:, 2, :], NR[:, :], SH[:, 1, :], ALU.subtract).then_inc(A.cols, 1)
                    elif kind == "shift":
                        dve.wait_ge(A.filled, pos + 1)
                        if not (isinstance(h, int) and h < 0):
                            dve.wait_ge(A.shift_loaded, (h + 1) * (16 * PARTS))
                        dve.tensor_copy(MT[:, :], slot[0:PARTS * TT, 0:P // 2].bitcast(BF16)).then_inc(A.freed, 1)
                    else:
                        dve.wait_ge(A.filled, pos + 1)
                        g = (h + ahead) * NQB + a
                        v = slot[:, 0:P].rearrange("p (t j) -> p t j", j=32)
                        dve.reciprocal(RC[:, a % 2, :, :], v[:, :, D:D + 1]).then_inc(A.sums, 1)
                        dve.wait_ge(A.sums, g + 1)
                        dve.tensor_tensor(AT[:, 4 * a:4 * a + 4, bass.ds((h + ahead) * D, D)], v[:, :, 0:D],
                                          RC[:, a % 2, :, :].to_broadcast([P, 4, D]), ALU.mult).then_inc(A.freed, 1)

                def step(h, c, turn):
                    whole = isinstance(h, int)
                    first = whole and h == 0
                    pos, bank, off = plan.ring_before(h), plan.static_before(h, c), 0
                    for b in range(plan.nb):
                        for item in plan.ring_items(b, h):
                            ring_item(item, pos + off, bank + off, h)
                            off += width(item)
                pos = 0
                for item in plan.prologue:
                    ring_item(item, pos, pos, -1)
                    pos += width(item)
                head_steps(dve, step)
                end = plan.ring_before(H)
                for q in range(NQB):
                    if plan.last_batch[q] + 3 >= plan.nb:
                        ring_item(("sum", q, 0, 0), end, end, H - 1)
                        end += 1

            def norms(call):
                for s in range(TT + 1):
                    if s < TT:
                        b = s % 2
                        y = X[:, s, :] if call < 2 else AT[:, s, :]
                        if call < 2:
                            dve.wait_ge(s_pj, call * TT + s + 1)
                            link(dve.tensor_tensor(y, B[2 + b][:, 0:C], y, ALU.add), s_ln)
                        link(dve.bn_stats(stats[:, b, :], y), s_ln)
                        link(dve.bn_aggr(agg[:, b, :], stats[:, b, :]), s_ln)
                        dve.tensor_scalar(var[:, b, 0:1], agg[:, b, 1:2], EPS, None, ALU.add).then_inc(s_var, 1)
                    if s >= 1:
                        t, b = s - 1, (s - 1) % 2
                        y = X[:, t, :] if call < 2 else AT[:, t, :]
                        dve.wait_ge(s_sd, call * TT + t + 1)
                        link(dve.reciprocal(var[:, b, 2:3], var[:, b, 1:2]), s_ln)
                        link(dve.scalar_tensor_tensor(out=var[:, b, 3:4], in0=var[:, b, 2:3], scalar=var[:, b, 2:3],
                                                      in1=var[:, b, 0:1], op0=ALU.mult, op1=ALU.mult), s_ln)
                        link(dve.tensor_scalar(var[:, b, 3:4], var[:, b, 3:4], -0.5, 1.5, ALU.mult, ALU.add), s_ln)
                        link(dve.tensor_tensor(var[:, b, 4:5], var[:, b, 2:3], var[:, b, 3:4], ALU.mult), s_ln)
                        dve.tensor_scalar(X[:, t, :], y, agg[:, b, 0:1], var[:, b, 4:5], ALU.subtract, ALU.mult).then_inc(s_xn, 1)

            attention(SA, SELF)
            norms(0)
            prep(PREP2, NPREP)
            attention(XA, CROSS)
            norms(1)

            gc = [0]

            def glink(ins):
                gc[0] += 1
                ins.then_inc(s_gc, 1)
                dve.wait_ge(s_gc, gc[0])
            dve.wait_ge(s_log, 1)
            dve.tensor_copy(L[:, :, :], B[4][:, 0:TT * E].rearrange("p (t e) -> p t e", e=E)).then_inc(s_gl, 1)
            dve.wait_ge(s_gl, 1)
            glink(dve.tensor_reduce(top[:, :, 0], L[:, :, :], AX.X, ALU.max))
            glink(dve.tensor_tensor(cmp_[:, :, :], L[:, :, :], top[:, :, :].to_broadcast([P, TT, E]), ALU.subtract))
            glink(dve.memset(rank[:, :, :], 0.0))
            for j in range(E):
                lj = L[:, :, j:j + 1]
                if j + 1 < E:
                    glink(dve.tensor_tensor(beat[:, :, j + 1:E], lj.to_broadcast([P, TT, E - 1 - j]), L[:, :, j + 1:E], ALU.is_ge))
                glink(dve.tensor_tensor(beat[:, :, 0:j + 1], lj.to_broadcast([P, TT, j + 1]), L[:, :, 0:j + 1], ALU.is_gt))
                glink(dve.tensor_tensor(rank[:, :, :], rank[:, :, :], beat[:, :, :], ALU.add))
            glink(dve.tensor_scalar(rank[:, :, :], rank[:, :, :], 2.0, None, ALU.is_lt))
            dve.wait_ge(s_ge, 1)
            glink(dve.tensor_tensor(G[:, :, :], G[:, :, :], rank[:, :, :], ALU.mult))
            glink(dve.tensor_reduce(top[:, :, 0], G[:, :, :], AX.X, ALU.add))
            glink(dve.reciprocal(top[:, :, :], top[:, :, :]))
            dve.tensor_tensor(G[:, :, :], G[:, :, :], top[:, :, :].to_broadcast([P, TT, E]), ALU.mult).then_inc(s_g, 1)

            for t in range(TT):
                dve.wait_ge(s_b2, t + 1)
                dve.tensor_tensor(AT[:, t, :], O[t % 2][:, 0:C], X[:, t, :], ALU.add).then_inc(s_acc0, 1)
            dve.wait_ge(s_acc0, TT)
            dve.wait_ge(s_g, 1)
            OB = B[4:8]
            with dve.Fori(0, E) as e:
                for t in range(TT):
                    dve.wait_ge(s_moe, e * TT + (t + 1 + 8))
                    dve.scalar_tensor_tensor(out=AT[:, t, :], in0=OB[t % 4][:, 0:C], scalar=G[:, t, bass.ds(e, 1)],
                                             in1=AT[:, t, :], op0=ALU.mult, op1=ALU.add).then_inc(s_moef, 1)
            dve.wait_ge(s_moef, 4 + E * TT)
            norms(2)


def _tables():
    def bf(v):
        return (np.ascontiguousarray(v, dtype=np.float32).view(np.uint32) >> 16).astype(np.uint16)
    pos = np.arange(N)
    inv = (np.float32(1.0) / np.float32(10000.0) ** (np.arange(0, D, 2, dtype=np.float32) / np.float32(D))).astype(np.float32)
    freqs = (pos.astype(np.float32)[:, None] * inv[None, :]).astype(np.float32)
    cos, sin = np.cos(freqs).T, np.sin(freqs).T
    root = np.float32(SCALE ** 0.5)
    cosT = np.tile(np.concatenate([cos, cos]), (P // D, 1)).astype(np.float32) * root
    sinT = np.tile(np.concatenate([-sin, sin]), (P // D, 1)).astype(np.float32) * root
    hi, lo = pos // P * P, pos % P
    q = np.zeros((S0, N), np.float32)
    kl = np.zeros((S0, N), np.float32)
    for s in range(PARTS):
        q[4 * s + 1], q[4 * s + 3] = -hi, -lo
        kl[4 * s], kl[4 * s + 2] = hi, lo
    q[MASK_ROW] = 1.0
    qx = np.zeros((S0, N), np.float32)
    qx[MASK_ROW] = 1.0
    sel = np.zeros((P, D + 1), np.float32)
    for g in range(4):
        sel[32 * g + np.arange(D + 1), np.arange(D + 1)] = 1.0
    j = np.arange(P)
    dist = np.minimum(j[None, :] - j[:, None], 0)
    pick = np.zeros((6 * H, PARTS), np.float32)
    pick[np.arange(6 * H), np.arange(6 * H) % 6 // 2] = 1.0
    return {
        "cosT": cosT, "sinT": sinT, "constQ": bf(q), "constQX": bf(qx), "constKL": bf(kl),
        "constK0": bf(np.zeros((S0, N))), "ones3": bf(np.ones((PARTS, N))), "ident": np.eye(P, dtype=np.float32),
        "identb": bf(np.eye(P)), "dist": bf(dist), "distT": bf(dist.T), "sel": sel, "pick": pick,
    }


def kernel(**inputs):
    import concourse.bacc as _bacc
    from concourse.bass_utils import run_bass_kernel_spmd as _run

    i = {k: np.asarray(v) for k, v in inputs.items()}
    qkv = i["L0_attn_qkv_w"]
    rot = np.arange(2 * C).reshape(-1, 2, D // 2)[:, ::-1].reshape(-1)
    a = {
        "x": i["x"][0], "xT": i["x"][0].T, "ctxT": i["ctx_1024"][0].T,
        "mask": i["mask_Bx1x1xS2_bf1"].reshape(1, NX).view(np.uint8),
        "wqkvT": qkv.T, "wrotT": qkv[rot].T, "wpT": i["L0_attn_proj_w"].T, "bp": i["L0_attn_proj_b"],
        "slopes": i["L0_attn_slopes"], "xwqT": i["L0_xattn_Wq"].T, "xwkT": i["L0_xattn_Wk"].T,
        "xwvT": i["L0_xattn_Wv"].T, "xwoT": i["L0_xattn_Wo"].T, "rT": i["L0_ffn_router_w"].T,
        "w1T": i["L0_ffn_w1"].transpose(0, 2, 1).reshape(E * C, F),
        "b1T": i["L0_ffn_b1"].reshape(E * FT, P).T,
        "w2T": i["L0_ffn_w2"].transpose(0, 2, 1).reshape(E * F, C), "b2": i["L0_ffn_b2"],
    }
    a.update(_tables())
    nc = _bacc.Bacc("TRN2", target_bir_lowering=False, num_devices=1)
    arrays, aps = {}, {}
    for name, v in a.items():
        v = np.ascontiguousarray(v)
        arrays[f"in_{name}_dram"] = v
        aps[name] = nc.dram_tensor(f"in_{name}_dram", v.shape, mybir.dt.from_np(v.dtype), kind="ExternalInput").ap()
        if v.dtype == np.uint16:
            aps[name] = aps[name].bitcast(BF16)
    aps["out"] = nc.dram_tensor("out_0_dram", (1, N, C), F32, kind="ExternalOutput").ap().rearrange("o n c -> (o n) c")
    layer(nc, **aps)
    r = _run(nc, [arrays], core_ids=[0])
    return r.results[0]["out_0_dram"]
```

```python
from contextlib import ExitStack

import concourse.bass as bass
from concourse import mybir
import numpy as np

ALU = mybir.AluOpType
ACT = mybir.ActivationFunctionType
AX = mybir.AxisListType
F32 = mybir.dt.float32
F32R = mybir.dt.float32r
BF16 = mybir.dt.bfloat16
U8 = mybir.dt.uint8

P = 128
N = 2048
C = 256
CT = C // P
H = 16
D = C // H
NX = 1601
NXP = -(-NX // P) * P
TT = N // P
QB = 512
NQB = N // QB
E = 8
F = 1024
FT = F // P
TB = 256
NTB = N // TB
PB = FT // 2
WN = CT * F + FT * C
PIECE = 512
NPIECE = WN // PIECE
PARTS = 3
PAIRS = 6
BIAS_ROWS = 12
MASK_ROW = 12
S0 = 13
A_ROWS = S0 + PAIRS * D
B_ROWS = A_ROWS + PARTS
SUM_LAG = 4
LEAD = 3
RING = 3
PRING = 12
SBANKS = 3
RBANKS = 3
MASKED = -1.0e38
SCALE = float(D) ** -0.5
MAX_BIAS = 8.0
EPS = 1e-5
HEADS_LOOPED = 12


class Plan:

    def __init__(self, nk, keys):
        self.nk = nk
        self.keys = keys
        self.chunk = keys // 4
        self.nu = NQB * nk
        self.nb = self.nu // 4
        self.last_batch = [((q + 1) * nk - 1) // 4 for q in range(NQB)]
        self.tail = [q for q in range(NQB) if self.last_batch[q] + SUM_LAG >= self.nb]
        self.per = -(-4 * TT // self.nb)
        self.early = min(LEAD * self.per, 4 * TT)
        self.prologue = self.chunks(0, 4 * TT, 1) + [("shift", 0, 0, 1)] + self.chunks(0, self.early, 2)

    def chunks(self, first, end, ahead):
        return [("max", n // 4, n % 4, ahead) for n in range(first, end)]

    def ring_items(self, b, h):
        whole = isinstance(h, int)
        items = []
        for q in range(NQB):
            at = self.last_batch[q] + SUM_LAG
            if at == b:
                items.append(("sum", q, 0, 0))
            if at - self.nb == b and not (whole and h == 0):
                items.append(("sum", q, 0, -1))
        slot = b + LEAD
        if slot < self.nb:
            if not (whole and h + 1 >= H):
                items += self.chunks(self.per * slot, min(self.per * (slot + 1), 4 * TT), 1)
        elif not (whole and h + 2 >= H):
            slot -= self.nb
            items += self.chunks(self.per * slot, self.per * (slot + 1), 2)
        if b == self.nb - LEAD + 1 and not (whole and h + 1 >= H):
            items.insert(2, ("shift", 0, 0, 1))
        return items

    def saves(self, b, first):
        out = []
        for q in range(NQB):
            at = self.last_batch[q] + 2
            if at == b:
                out.append((q, 0))
            if at - self.nb == b and not first:
                out.append((q, -1))
        return out

    def used(self, items):
        return sum(width(i) for i in items)

    def head_items(self, h):
        return [i for b in range(self.nb) for i in self.ring_items(b, h)]

    def ring_before(self, h):
        if isinstance(h, int):
            return self.used(self.prologue) + sum(self.used(self.head_items(g)) for g in range(h))
        each = self.used(self.head_items(1))
        return h * each + (self.ring_before(1) - each)

    def static_before(self, h, c):
        assert RING * self.used(self.head_items(1)) % RBANKS == 0
        return self.ring_before(h if isinstance(h, int) else (c if c else RING))

    def shift_end(self, h):
        if isinstance(h, int) and h == 0:
            return 4 * TT + 1
        before = h - 1
        items = self.head_items(before if isinstance(before, int) else 1)
        at = [i[0] for i in items].index("shift")
        return self.ring_before(before) + self.used(items[:at + 1])


def width(item):
    return 1


SELF = Plan(TT, N)
CROSS = Plan(NXP // P, NXP)


def layer(nc, x, xT, ctxT, mask, wqkvT, wrotT, wpT, bp, slopes, xwqT, xwkT, xwvT, xwoT, rT, w1T, b1T, w2T, b2,
          cosT, sinT, constQ, constQX, constKL, constK0, ones3, ident, identb, dist, distT, sel, pick, out):
    with ExitStack() as ctx:
        def sb(name, shape, dt=F32):
            return ctx.enter_context(nc.sbuf_tensor(name, shape, dt))

        def ps(name, shape, dt=F32):
            return ctx.enter_context(nc.psum_tensor(name, shape, dt))

        def sem(name):
            return ctx.enter_context(nc.semaphore(name))

        X = sb("X", [P, TT, C])
        AT = sb("AT", [P, TT, C])
        XT = sb("XT", [P, CT, N])
        xwo = sb("xwo", [P, CT, C])
        b2S = sb("b2S", [E, C])
        b1S = sb("b1S", [P, E * FT])
        b1E = sb("b1E", [P, 2, FT])
        rS = sb("rS", [P, CT, E])
        idf = sb("idf", [P, P])
        ATT = sb("ATT", [P, 2, CT, P])
        stats = sb("stats", [P, 2, 6])
        agg = sb("agg", [P, 2, 2])
        var = sb("var", [P, 2, 5])
        G = sb("G", [P, TT, E])
        top = sb("top", [P, TT, 1])
        persistent, sb = sb, lambda name, shape, dt=F32: attention_memory.enter_context(nc.sbuf_tensor(name, shape, dt))
        attention_memory = ExitStack()
        arena = sb("arena", [P, (TT + NXP // P) * C + CT * NXP])
        VA = arena[:, 0:TT * C].rearrange("p (t c) -> p t c", c=C)
        VX = arena[:, TT * C:(TT + NXP // P) * C].rearrange("p (t c) -> p t c", c=C)
        CX = arena[:, (TT + NXP // P) * C:].rearrange("p (k n) -> p k n", k=CT)
        oper = sb("oper", [P, RING * 3 * N], BF16)
        QO = oper[:, 0:RING * N].rearrange("p (r n) -> p r n", r=RING)
        KO = oper[:, RING * N:].rearrange("p (r v n) -> p r v n", r=RING, v=2)
        PT = sb("PT", [P, PRING, QB])
        flatPT = PT[:, :, :].rearrange("p a b -> p (a b)")
        cosS = flatPT[:, 0:N]
        sinS = flatPT[:, N:2 * N]
        OH = sb("OH", [P, 2, QB], F32R)
        OL = sb("OL", [P, 2, QB], F32R)
        VS = sb("VS", [P, RING, TT, 2 * D])
        SD = sb("SD", [P, RING, PARTS, P], BF16)
        flatAT = AT[:, :, :].rearrange("p t c -> p (t c)")
        T1 = flatAT[:, 0:2 * QB].rearrange("p (b n) -> p b n", b=2)
        T2 = flatAT[:, 2 * QB:4 * QB].rearrange("p (b n) -> p b n", b=2)
        slopeF = flatAT[0:6 * H, 4 * QB:4 * QB + N // 2].bitcast(BF16)
        QF = flatPT[:, 2 * N:2 * N + 3 * QB].rearrange("p (b n) -> p b n", b=3)
        RF = flatAT[:, 6 * QB:8 * QB].rearrange("p (b n) -> p b n", b=2)
        parts = sb("parts", [P, 3, PARTS, QB], BF16)
        wqkv = sb("wqkv", [P, CT, 3 * C])
        wrot = sb("wrot", [P, CT, 2 * C])
        OS = wrot
        wp = sb("wp", [P, CT, C])
        xwq = sb("xwq", [P, CT, C])
        xwk = sb("xwk", [P, CT, C])
        xwv = sb("xwv", [P, CT, C])
        bpS = sb("bpS", [P, C])
        idb = sb("idb", [P, P], BF16)
        dS = sb("dS", [P, P], BF16)
        dTS = sb("dTS", [P, P], BF16)
        selS = sb("selS", [P, D + 2])
        selR = sb("selR", [P, D + 2], F32R)
        slB = sb("slB", [P, H])
        scratch = flatPT[:, 2 * N + 3 * QB:2 * N + 4 * QB]
        mU8 = scratch[0:1, 0:(NX + 3) // 4].bitcast(U8)[:, 0:NX]
        sl8, slR = (scratch[:, QB - (i + 1) * H:QB - i * H] for i in range(2))
        slPF = scratch[:, QB - 5 * H:QB - 2 * H].rearrange("p (s h) -> p s h", h=H)
        slP = sb("slP", [P, PARTS, H], BF16)
        slopeDiag = sb("slopeDiag", [P, 2, PARTS, P], BF16)
        slRow = sb("slRow", [6 * H, 8])
        slRowB = sb("slRowB", [6 * H, 4], BF16)
        mRow = sb("mRow", [1, NXP], BF16)
        CM = sb("CM", [P, TT, 4])
        NM = sb("NM", [P, TT])
        NR = sb("NR", [P, TT])
        SHW = sb("SHW", [P, P], BF16)
        SH = SHW[:, 0:PARTS * TT].rearrange("p (s t) -> p s t", t=TT)
        MT = sb("MT", [PARTS * TT, P], BF16)
        RC = sb("RC", [P, 2, 4, 1])
        one = sb("one", [P, 1])
        pickS = sb("pickS", [6 * H, PARTS])
        attention_memory.close()
        sb = persistent
        XH = sb("XH", [P, CT, N], F32R)
        XL = sb("XL", [P, CT, N], F32R)
        WR = sb("WR", [P, WN])
        WH = sb("WH", [P, 2, WN], F32R)
        WL = sb("WL", [P, 2, WN], F32R)
        GR = sb("GR", [P, PB, 2, TB])
        HH = sb("HH", [P, 2, FT, TB], F32R)
        HL = sb("HL", [P, 2, FT, TB], F32R)
        L, rank, cmp_, beat = (GR[:, i, 0, 0:TT * E].rearrange("p (t e) -> p t e", e=E) for i in range(4))
        GT = GR[0:E, :, :, :].rearrange("p a b c -> p (a b c)")

        B = [ps(f"B{i}", [P, QB]) for i in range(8)]
        S = B[0:SBANKS]
        R = B[SBANKS:SBANKS + RBANKS]
        O = B[6:8]

        qD = nc.dram_tensor("qD", [PARTS, C, N], BF16).ap()
        kD = nc.dram_tensor("kD", [PARTS, C, N], BF16).ap()
        qxD = nc.dram_tensor("qxD", [PARTS, C, N], BF16).ap()
        kxD = nc.dram_tensor("kxD", [PARTS, C, NXP], BF16).ap()
        slD = nc.dram_tensor("slD", [6 * H, N], BF16).ap()
        sdD = nc.dram_tensor("sdD", [H * P, PARTS * P], BF16).ap()

        s_w = sem("weights_loaded")
        s_x = sem("stream_loaded")
        s_c = sem("context_loaded")
        s_k = sem("constants_loaded")
        s_selr = sem("group_sums_ready")
        s_rope = sem("rope_tables_loaded")
        s_m = sem("misc_constants_loaded")
        s_zero = sem("buffers_cleared")
        s_prep = sem("proj_ready")
        s_prepfree = sem("proj_read")
        s_chain = sem("slope_chain")
        s_q = sem("prep_value_ready")
        s_hi = sem("prep_high_ready")
        s_r = sem("prep_rest_ready")
        s_mi = sem("prep_middle_ready")
        s_lo = sem("prep_parts_ready")
        s_st = [sem(f"parts_stored{i}") for i in range(3)]
        s_v = sem("v_proj_ready")
        s_vs = sem("v_proj_saved")
        s_sl = sem("slope_rows_ready")
        s_slout = sem("slope_rows_stored")
        s_sdr = sem("slope_diag_ready")
        s_sdo = [sem(f"slope_diag_stored{i}") for i in range(2)]
        s_mask = sem("mask_row_ready")
        s_mrow = sem("mask_row_placed")
        s_const = sem("constant_rows_placed")
        s_tr = sem("attention_transposed")
        s_att = sem("attention_transpose_saved")
        s_pj = sem("output_projected")
        s_ln = sem("norm_chain")
        s_var = sem("variance_ready")
        s_sd = sem("deviation_ready")
        s_xn = sem("stream_normed")
        s_xt = sem("stream_transposed")
        s_xts = sem("stream_transpose_saved")
        s_log = sem("logits_ready")
        s_gl = sem("logits_saved")
        s_gc = sem("gate_chain")
        s_ge = sem("gate_exp")
        s_g = sem("gates_ready")
        s_gt = sem("gates_transposed")
        s_gts = sem("gates_transpose_saved")
        s_b2 = sem("bias_mix_ready")
        s_acc0 = sem("experts_sum_started")
        s_raw = sem("expert_weights_loaded")
        s_w0h = sem("first_weights_high")
        s_w0 = sem("first_weights_split")
        s_wh = sem("weights_high_ready")
        s_ws = sem("weights_split")
        s_xh = sem("stream_high_ready")
        s_xl = sem("stream_split")
        s_hh = sem("hidden_high_ready")
        s_hs = sem("hidden_split")
        s_hid = sem("hidden_ready")
        s_gelu = sem("gelu_done")
        s_b1 = sem("expert_bias_ready")
        s_moe = sem("expert_ready")
        s_moef = sem("expert_added")
        s_out = sem("output_stored")

        class Att:
            def __init__(self, name):
                self.loaded = [sem(f"{name}_operands_loaded{i}") for i in range(RING)]
                self.shift_loaded = sem(f"{name}_shift_loaded")
                self.scores = sem(f"{name}_scores_ready")
                self.exps = sem(f"{name}_exps_done")
                self.pv = sem(f"{name}_pv_done")
                self.saved = sem(f"{name}_acc_saved")
                self.high = sem(f"{name}_acc_high_ready")
                self.split = sem(f"{name}_acc_split")
                self.filled = sem(f"{name}_ring_filled")
                self.freed = sem(f"{name}_ring_freed")
                self.sums = sem(f"{name}_sums_taken")
                self.v = sem(f"{name}_v_staged")
                self.chain = sem(f"{name}_shift_chain")
                self.cols = sem(f"{name}_shift_cols_ready")
        SA, XA = Att("self"), Att("cross")

        block = ctx.enter_context(nc.Block())

        def items_of(kind, n):
            return [(kind, half, c * n, n) for half in range(CT) for c in range(4)]
        PREP1 = items_of("q", QB) + items_of("k", QB) + items_of("xk", NXP // 4)
        PREP2 = items_of("xq", QB)
        dest = {"q": qD, "k": kD, "xk": kxD, "xq": qxD}
        NPREP = len(PREP1)

        def head_steps(engine, body):
            body(0, 0, 0)
            with engine.Fori(0, HEADS_LOOPED // RING) as it:
                for c in range(RING):
                    h = it * RING + (1 + c)
                    body(h, (1 + c) % RING, it + (1 + c) // RING)
            for h in range(HEADS_LOOPED + 1, H):
                body(h, h % RING, h // RING)

        def expert_steps(engine, body):
            body(0, 0)
            with engine.Fori(0, E // 2 - 1) as it:
                body(it * 2 + 1, 1)
                body(it * 2 + 2, 0)
            body(E - 1, 1)

        @block.sync
        def _(sp):
            sp.dma_start(XT[:, :, :], xT.rearrange("(k p) n -> p k n", p=P)).then_inc(s_x, 16)
            sp.dma_start(wqkv[:, :, :], wqkvT.rearrange("(k p) n -> p k n", p=P)).then_inc(s_w, 16)
            sp.dma_start(wrot[:, :, :], wrotT.rearrange("(k p) n -> p k n", p=P)).then_inc(s_w, 16)
            sp.dma_start(cosS, cosT).then_inc(s_rope, 16)
            sp.dma_start(sinS, sinT).then_inc(s_rope, 16)
            sp.dma_start(CX[:, :, 0:NX], ctxT.rearrange("(k p) n -> p k n", p=P)).then_inc(s_c, 16)
            for w, src in ((xwk, xwkT), (xwv, xwvT), (xwq, xwqT), (wp, wpT), (xwo, xwoT)):
                sp.dma_start(w[:, :, :], src.rearrange("(k p) n -> p k n", p=P)).then_inc(s_c, 16)
            sp.dma_start(X[:, :, :], x.rearrange("(t p) c -> p t c", p=P)).then_inc(s_m, 16)
            sp.dma_start(bpS[:, :], bp.partition_broadcast(P)).then_inc(s_m, 16)
            sp.dma_start(b2S[:, :], b2).then_inc(s_m, 16)
            sp.dma_start(b1S[:, :], b1T).then_inc(s_m, 16)
            sp.dma_start(rS[:, :, :], rT.rearrange("(k p) n -> p k n", p=P)).then_inc(s_m, 16)
            for r in range(RING):
                sp.dma_start(QO[0:S0, r, :], constQ).then_inc(s_const, 16)
                sp.dma_start(KO[0:S0, r, 0, :], constKL).then_inc(s_const, 16)
                sp.dma_start(KO[0:S0, r, 1, :], constK0).then_inc(s_const, 16)
                for v in range(2):
                    sp.dma_start(KO[A_ROWS:B_ROWS, r, v, :], ones3).then_inc(s_const, 16)

            def store_parts(items, first):
                for n, (kind, half, c0, w) in enumerate(items):
                    i = first + n
                    sp.wait_ge(s_lo, i + 1)
                    sp.dma_start(dest[kind][:, half * P:(half + 1) * P, c0:c0 + w].rearrange("s r c -> r s c"),
                                 parts[:, i % 3, :, 0:w]).then_inc(s_st[i % 3], 16)

            store_parts(PREP1[0:16], 0)
            sp.wait_ge(s_sl, 1)
            sp.dma_start(slD, slopeF).then_inc(s_slout, 16)
            for h in range(H):
                sp.wait_ge(s_sdr, h + 1)
                sp.dma_start(sdD[h * P:(h + 1) * P, :], slopeDiag[:, h % 2, :, :].rearrange("p s j -> p (s j)")).then_inc(s_sdo[h % 2], 16)
            store_parts(PREP1[16:], 16)
            for i in range(3):
                sp.wait_ge(s_st[i], 16 * (NPREP // 3))
            sp.wait_ge(s_slout, 16)
            sp.wait_ge(s_sdo[0], 16 * H // 2)
            sp.wait_ge(s_sdo[1], 16 * H // 2)
            sp.wait_ge(s_const, 16 * 5 * RING)

            def attention_loads(A, plan, qsrc, ksrc):
                alibi = A is SA

                def load(h, c):
                    rows = bass.ds(h * D, D)
                    q = QO[S0:A_ROWS, c, :]
                    ld = A.loaded[c]
                    sp.dma_start(q[0:3 * D, :], qsrc[0:3, rows, :]).then_inc(ld, 16)
                    sp.dma_start(q[3 * D:5 * D, :], qsrc[0:2, rows, :]).then_inc(ld, 16)
                    sp.dma_start(q[5 * D:6 * D, :], qsrc[0, rows, :]).then_inc(ld, 16)
                    for v in range(2 if alibi else 1):
                        k = KO[S0:A_ROWS, c, v, 0:plan.keys]
                        row = 0
                        for part, times in ((0, 3), (1, 2), (2, 1)):
                            sp.dma_start(k[row:row + times * D, :],
                                         ksrc[part:part + 1, rows, :].to_broadcast([times, D, plan.keys])).then_inc(ld, 16)
                            row += times * D
                    if alibi:
                        srows = bass.ds(h * 6, 6)
                        sp.dma_start(QO[0:BIAS_ROWS:2, c, :], slD[srows, :]).then_inc(ld, 16)
                        sp.dma_start(KO[1:BIAS_ROWS:2, c, 0, :], slD[srows, :]).then_inc(ld, 16)
                        sp.dma_start(SD[:, c, :, :].rearrange("p s j -> p (s j)"), sdD[bass.ds(h * P, P), :]).then_inc(ld, 16)

                def place_shift(h, c):
                    sp.wait_ge(A.freed, plan.shift_end(h))
                    for s in range(PARTS):
                        sp.dma_start(QO[A_ROWS + s:A_ROWS + s + 1, c, :],
                                     MT[s * TT:(s + 1) * TT, :]).then_inc(A.shift_loaded, 16)

                for h in range(RING):
                    load(h, h)
                place_shift(0, 0)

                def step(h, c, turn):
                    whole = isinstance(h, int)
                    if not (whole and (h == 0 or h + 2 >= H)):
                        sp.wait_ge(A.scores, plan.nu * h)
                        load(h + 2, (c + 2) % RING)
                    if not (whole and h + 1 >= H):
                        place_shift(h + 1, (c + 1) % RING)
                head_steps(sp, step)

            attention_loads(SA, SELF, qD, kD)
            sp.wait_ge(SA.scores, SELF.nu * H)
            for r in range(RING):
                sp.dma_start(QO[0:S0, r, :], constQX).then_inc(s_mrow, 16)
                sp.dma_start(KO[0:BIAS_ROWS, r, 0, :], constK0[0:BIAS_ROWS, :]).then_inc(s_mrow, 16)
                if r == 0:
                    sp.wait_ge(s_mask, 2)
                sp.dma_start(KO[MASK_ROW:MASK_ROW + 1, r, 0, 0:NXP], mRow[:, :]).then_inc(s_mrow, 16)
            store_parts(PREP2, NPREP)
            for i in range(3):
                sp.wait_ge(s_st[i], 16 * ((NPREP + len(PREP2) - i + 2) // 3))
            attention_loads(XA, CROSS, qxD, kxD)

            def load_weights(e):
                sp.dma_start(WR[:, 0:CT * F].rearrange("p (k f) -> p k f", k=CT),
                             w1T[bass.ds(e * C, C), :].rearrange("(k p) f -> p k f", p=P)).then_inc(s_raw, 16)
                sp.dma_start(WR[:, CT * F:WN].rearrange("p (f c) -> p f c", f=FT),
                             w2T[bass.ds(e * F, F), :].rearrange("(f p) c -> p f c", p=P)).then_inc(s_raw, 16)
            sp.wait_ge(s_tr, TT + 1)
            load_weights(0)
            sp.wait_ge(s_w0, NPIECE)
            load_weights(1)
            with sp.Fori(2, E) as e:
                sp.wait_ge(s_ws, (e - 1) * NPIECE)
                load_weights(e)
            for t in range(TT):
                sp.wait_ge(s_xn, 2 * TT + t + 1)
                sp.dma_start(out[t * P:(t + 1) * P, :], X[:, t, :]).then_inc(s_out, 16)
            sp.wait_ge(s_out, 16 * TT)

        @block.gpsimd
        def _(pool):
            pool.dma_start(slB[:, :], slopes.partition_broadcast(P)).then_inc(s_k, 16)
            pool.dma_start(slRow[:, 0:1],
                           slopes.rearrange("(h s o) -> h s o", s=1, o=1).to_broadcast([H, 6, 1])).then_inc(s_k, 16)
            pool.dma_start(mU8[:, :], mask).then_inc(s_k, 16)
            for dst, src in ((idf, ident), (idb, identb), (dS, dist), (dTS, distT), (selS, sel), (pickS, pick)):
                pool.dma_start(dst[:, :], src).then_inc(s_k, 16)
            pool.memset(CX[:, :, NX:NXP], 0.0).then_inc(s_zero, 1)
            pool.memset(VS[:, :, :, D:2 * D], 0.0).then_inc(s_zero, 1)
            pool.wait_ge(s_zero, 2)
            pool.memset(VS[:, :, :, D:D + 1], 1.0).then_inc(s_zero, 1)
            pool.memset(one[:, :], 1.0).then_inc(s_zero, 1)
            pool.wait_ge(s_zero, 4)

            def attention(A, plan, V):
                nk = plan.nk

                def stage(h, c):
                    pool.tensor_copy(VS[:, c, 0:nk, 0:D], V[:, 0:nk, bass.ds(h * D, D)]).then_inc(A.v, 1)

                def split(q, h):
                    g = h * NQB + (q + 1)
                    pool.wait_ge(A.saved, g)
                    pool.tensor_tensor(OH[:, q % 2, :], OS[:, q % 2, :], one[:, :].to_broadcast([P, QB]), ALU.mult).then_inc(A.high, 1)
                    pool.wait_ge(A.high, g)
                    pool.tensor_tensor(OL[:, q % 2, :], OS[:, q % 2, :], OH[:, q % 2, :].bitcast(F32),
                                       ALU.subtract).then_inc(A.split, 1)

                def step(h, c, turn):
                    whole = isinstance(h, int)
                    if not (whole and h == 0):
                        split(NQB - 1, h - 1)
                    if not (whole and (h == 0 or h + 2 >= H)):
                        pool.wait_ge(A.pv, plan.nb * h)
                        stage(h + 2, (c + 2) % RING)
                    for q in range(NQB - 1):
                        split(q, h)
                for h in range(RING):
                    stage(h, h)
                head_steps(pool, step)
                split(NQB - 1, H - 1)
            pool.wait_ge(s_k, 16 * 9)
            pool.wait_ge(s_vs, TT)
            pool.tensor_copy(selR[:, :], selS[:, :]).then_inc(s_selr, 1)
            attention(SA, SELF, VA)
            pool.wait_ge(s_vs, TT + NXP // P)
            pool.wait_ge(SA.pv, SELF.nb * H)
            attention(XA, CROSS, VX)

            pool.wait_ge(s_tr, TT + 1)
            for t in range(TT):
                at = slice(t * P, (t + 1) * P)
                pool.wait_ge(s_xts, TT + t + 1)
                pool.tensor_copy(XH[:, :, at], XT[:, :, at]).then_inc(s_xh, 1)
                pool.wait_ge(s_xh, t + 1)
                pool.tensor_tensor(XL[:, :, at], XT[:, :, at], XH[:, :, at].bitcast(F32), ALU.subtract).then_inc(s_xl, 1)
                n = t - (TT - NPIECE)
                if n >= 0:
                    if n == 0:
                        pool.wait_ge(s_raw, 32)
                    w = slice(n * PIECE, (n + 1) * PIECE)
                    pool.tensor_copy(WH[:, 0, w], WR[:, w]).then_inc(s_w0h, 1)
                    pool.wait_ge(s_w0h, n + 1)
                    pool.tensor_tensor(WL[:, 0, w], WR[:, w], WH[:, 0, w].bitcast(F32), ALU.subtract).then_inc(s_w0, 1)

        @block.tensor
        def _(pe):
            def prep(items, first):
                for n, (kind, half, c0, w) in enumerate(items):
                    i = first + n
                    wt, off = {"q": (wqkv, 0), "k": (wqkv, C), "xk": (xwk, 0), "xq": (xwq, 0)}[kind]
                    src = CX if kind == "xk" else XT
                    if i >= 2:
                        pe.wait_ge(s_prepfree, i - 1)
                    for k in range(CT):
                        mm = pe.matmul(B[2 * (i % 2)][:, 0:w], wt[:, k, off + half * P:off + (half + 1) * P],
                                       src[:, k, c0:c0 + w], start=(k == 0), stop=(k == CT - 1))
                    if kind in "qk":
                        for k in range(CT):
                            mm = pe.matmul(B[2 * (i % 2) + 1][:, 0:w], wrot[:, k, off + half * P:off + (half + 1) * P],
                                           src[:, k, c0:c0 + w], start=(k == 0), stop=(k == CT - 1))
                    mm.then_inc(s_prep, 1)

            def v_proj(src, wt, off, n, first):
                for t in range(n):
                    i = first + t
                    if i >= 2:
                        pe.wait_ge(s_vs, i - 1)
                    for k in range(CT):
                        mm = pe.matmul(B[4 + i % 2][:, 0:C], src[:, k, t * P:(t + 1) * P], wt[:, k, off:off + C],
                                       start=(k == 0), stop=(k == CT - 1))
                    mm.then_inc(s_v, 1)

            pe.wait_ge(s_x, 16)
            pe.wait_ge(s_w, 32)
            prep(PREP1[0:16], 0)
            v_proj(XT, wqkv, 2 * C, TT, 0)
            pe.wait_ge(s_c, 16 * 6)
            pe.wait_ge(s_zero, 4)
            prep(PREP1[16:], 16)
            v_proj(CX, xwv, 0, NXP // P, TT)

            def attention(A, plan):
                alibi = A is SA
                nk, ch = plan.nk, plan.chunk

                def ring_item(item, pos, bank, h, c):
                    kind, a, b, ahead = item
                    if not isinstance(pos, int) or pos + width(item) > RBANKS:
                        pe.wait_ge(A.freed, pos + (width(item) - RBANKS))
                    slot = R[bank % RBANKS]
                    if kind == "max":
                        t, k0, k1 = a, b * ch, (b + 1) * ch
                        c2 = (c + ahead) % RING
                        if a == 0 and b == 0:
                            pe.wait_ge(A.loaded[c2], loads_due(h, c, ahead))
                        q = QO[0:A_ROWS, c2, t * P:(t + 1) * P]
                        low = min(max(t * P, k0), k1) - k0 if alibi else ch
                        diag = alibi and k0 <= t * P < k1
                        if low:
                            mm = pe.matmul(slot[:, 0:low], q, KO[0:A_ROWS, c2, 0, k0:k0 + low],
                                           start=True, stop=True, skip_group_check=True)
                        if low < ch:
                            mm = pe.matmul(slot[:, low:ch], q, KO[0:A_ROWS, c2, 1, k0 + low:k1],
                                           start=(low == 0), stop=not diag, skip_group_check=True)
                        if diag:
                            for s in range(PARTS):
                                mm = pe.matmul(slot[:, low:low + P], SD[:, c2, s, :], dS[:, :],
                                               start=False, stop=(s == PARTS - 1), skip_group_check=True)
                        mm.then_inc(A.filled, 1)
                    elif kind == "shift":
                        pe.wait_ge(A.cols, h + 2)
                        pe.transpose(slot[:, 0:P // 2].bitcast(BF16), SHW[:, :],
                                     idb[:, :]).then_inc(A.filled, 1)
                    else:
                        pe.wait_ge(A.split, (h + ahead) * NQB + (a + 1))
                        for t in range(4):
                            for part in (OH, OL):
                                mm = pe.matmul(slot[:, t * 32:t * 32 + D + 2], part[:, a % 2, t * P:(t + 1) * P], selR[:, :],
                                               start=(part is OH), stop=(part is OL), skip_group_check=True)
                        mm.then_inc(A.filled, 1)

                turn_now = [0]

                def loads_due(h, c, ahead):
                    per = 16 * (12 if alibi else 6)
                    if isinstance(h, int):
                        return per * ((h + ahead) // RING + 1)
                    return (turn_now[0] + ((c + ahead) // RING + 1)) * per

                def scores_unit(u, h, c):
                    qb, kt = u // nk, u % nk
                    if not (isinstance(h, int) and h == 0 and u < SBANKS):
                        pe.wait_ge(A.exps, plan.nu * h + (u + 1 - SBANKS))
                    bank = S[(c * plan.nu + u) % SBANKS]
                    q0 = qb * QB
                    lo = min(max(kt * P - q0, 0), QB) if alibi else 0
                    diag = alibi and q0 <= kt * P < q0 + QB
                    up = lo + P if diag else lo
                    stat = [KO[0:B_ROWS, c, v, kt * P:(kt + 1) * P] for v in range(2)]
                    if up:
                        mm = pe.matmul(bank[:, 0:up], stat[1], QO[0:B_ROWS, c, q0:q0 + up],
                                       start=True, stop=not diag, skip_group_check=True)
                    if diag:
                        for s in range(PARTS):
                            mm = pe.matmul(bank[:, lo:up], SD[:, c, s, :], dTS[:, :],
                                           start=False, stop=(s == PARTS - 1), skip_group_check=True)
                    if up < QB:
                        mm = pe.matmul(bank[:, up:QB], stat[0], QO[0:B_ROWS, c, q0 + up:q0 + QB],
                                       start=(up == 0), stop=True, skip_group_check=True)
                    mm.then_inc(A.scores, 1)

                def pv_batch(b, h, c):
                    pe.wait_ge(A.exps, plan.nu * h + (4 * b + 4))
                    for u in range(4 * b, 4 * b + 4):
                        qb, kt = u // nk, u % nk
                        if kt == 0 and not (isinstance(h, int) and h == 0 and qb < 2):
                            pe.wait_ge(A.saved, h * NQB + (qb - 1))
                        g = u % 4
                        mm = pe.matmul(O[qb % 2][32 * g:32 * g + 32, :], VS[:, c, kt, :],
                                       PT[:, (c * plan.nu + u) % PRING, :],
                                       start=(kt < 4), stop=(kt + 4 >= nk), skip_group_check=True)
                    mm.then_inc(A.pv, 1)

                def step(h, c, turn):
                    whole = isinstance(h, int)
                    first = whole and h == 0
                    turn_now[0] = turn
                    pos = plan.ring_before(h)
                    static = plan.static_before(h, c)
                    pe.wait_ge(A.shift_loaded, (h + 1) * 16 * PARTS)
                    off = 0

                    def ring(items):
                        nonlocal off
                        for item in items:
                            ring_item(item, pos + off, static + off, h, c)
                            off += width(item)
                    for b in range(plan.nb):
                        items = plan.ring_items(b, h)
                        cuts = [len(items) * n // 4 for n in range(5)]
                        for n in range(4):
                            scores_unit(4 * b + n, h, c)
                            ring(items[cuts[n]:cuts[n + 1]])
                            if n == 1 and b > 0:
                                pv_batch(b - 1, h, c)
                            elif n == 1:
                                if not first:
                                    pv_batch(plan.nb - 1, h - 1, (c - 1) % RING)
                                pe.wait_ge(A.v, h + 1)

                pos = 0
                for item in plan.prologue:
                    ring_item(item, pos, pos, -1, RING - 1)
                    pos += width(item)
                head_steps(pe, step)
                pv_batch(plan.nb - 1, H - 1, (H - 1) % RING)
                end = plan.ring_before(H)
                for q in plan.tail:
                    ring_item(("sum", q, 0, 0), end, end, H - 1, 0)
                    end += 1

            def project_norm(call, A, plan, w):
                pe.wait_ge(A.freed, plan.ring_before(H) + len(plan.tail))
                b0 = call * TT
                for s in range(TT + 3):
                    if s < TT:
                        if s >= 2:
                            pe.wait_ge(s_att, b0 + s - 1)
                        for k in range(CT):
                            mm = pe.transpose(B[s % 2][:, k * P:(k + 1) * P], AT[:, s, k * P:(k + 1) * P], idf[:, :])
                        mm.then_inc(s_tr, 1)
                    t = s - 1
                    if 0 <= t < TT:
                        pe.wait_ge(s_att, b0 + t + 1)
                        if t >= 2:
                            pe.wait_ge(s_xn, b0 + t - 1)
                        for k in range(CT):
                            mm = pe.matmul(B[2 + t % 2][:, 0:C], ATT[:, t % 2, k, :], w[:, k, :],
                                           start=(k == 0), stop=(k == CT - 1))
                        mm.then_inc(s_pj, 1)
                    t = s - 3
                    if 0 <= t < TT:
                        pe.wait_ge(s_xn, b0 + t + 1)
                        if t >= 2:
                            pe.wait_ge(s_xts, b0 + t - 1)
                        for k in range(CT):
                            mm = pe.transpose(O[t % 2][:, k * P:(k + 1) * P], X[:, t, k * P:(k + 1) * P], idf[:, :])
                        mm.then_inc(s_xt, 1)

            pe.wait_ge(s_prepfree, NPREP)
            pe.wait_ge(s_vs, TT + NXP // P)
            pe.wait_ge(s_selr, 1)
            pe.wait_ge(s_k, 16 * 9)
            pe.wait_ge(s_const, 16 * 5 * RING)
            attention(SA, SELF)
            project_norm(0, SA, SELF, wp)
            pe.wait_ge(s_xts, TT)
            pe.wait_ge(s_xn, TT)
            prep(PREP2, NPREP)
            pe.wait_ge(s_prepfree, NPREP + len(PREP2))
            pe.wait_ge(s_mrow, 16 * 3 * RING)
            attention(XA, CROSS)
            project_norm(1, XA, CROSS, xwo)

            pe.wait_ge(s_xts, 2 * TT)
            for t in range(TT):
                for k in range(CT):
                    mm = pe.matmul(B[4][:, t * E:(t + 1) * E], XT[:, k, t * P:(t + 1) * P], rS[:, k, :],
                                   start=(k == 0), stop=(k == CT - 1), skip_group_check=True)
            mm.then_inc(s_log, 1)
            pe.wait_ge(s_g, 1)
            for t in range(TT):
                mm = pe.transpose(B[t // 4][0:E, (t % 4) * P:(t % 4 + 1) * P], G[:, t, :], idf[:, :])
            mm.then_inc(s_gt, 1)
            pe.wait_ge(s_gts, 4)
            for t in range(TT):
                if t >= 2:
                    pe.wait_ge(s_acc0, t - 1)
                pe.matmul(O[t % 2][:, 0:C], GT[:, t * P:(t + 1) * P], b2S[:, :], start=True, stop=True).then_inc(s_b2, 1)
            pe.wait_ge(s_acc0, TT)

            HB, OB = B[0:4], B[4:8]

            def first_layer(e, b, blk):
                tok = slice(blk * TB, (blk + 1) * TB)
                for i in range(PB):
                    if not (isinstance(e, int) and e == 0 and blk == 0):
                        pe.wait_ge(s_gelu, e * (NTB * PB) + (blk * PB + i + 1 - PB))
                    for q in range(2):
                        f = 2 * i + q
                        n = 0
                        for k in range(CT):
                            w = slice(k * F + f * P, k * F + (f + 1) * P)
                            for wt, xt in ((WH, XH), (WH, XL), (WL, XH)):
                                mm = pe.matmul(HB[i][:, q * TB:(q + 1) * TB], wt[:, b, w], xt[:, k, tok],
                                               start=(n == 0), stop=(n == 3 * CT - 1), skip_group_check=True)
                                n += 1
                    mm.then_inc(s_hid, 1)

            def second_layer(e, b, blk):
                pe.wait_ge(s_hs, e * (NTB * PB) + (blk + 1) * PB)
                for j in range(2):
                    m = 2 * blk + j
                    if not (isinstance(e, int) and e == 0 and m < 4):
                        pe.wait_ge(s_moef, e * TT + (m + 1 - 4))
                    n = 0
                    for f in range(FT):
                        w = slice(CT * F + f * C, CT * F + (f + 1) * C)
                        for ht, wt in ((HH, WH), (HH, WL), (HL, WH)):
                            mm = pe.matmul(OB[m % 4][:, 0:C], ht[:, blk % 2, f, j * P:(j + 1) * P], wt[:, b, w],
                                           start=(n == 0), stop=(n == 3 * FT - 1))
                            n += 1
                    mm.then_inc(s_moe, 1)

            pe.wait_ge(s_xl, TT)

            def expert(e, b):
                first = isinstance(e, int) and e == 0
                if first:
                    pe.wait_ge(s_w0, NPIECE)
                else:
                    pe.wait_ge(s_ws, e * NPIECE)
                for blk in range(NTB):
                    first_layer(e, b, blk)
                    if blk:
                        second_layer(e, b, blk - 1)
                    elif not first:
                        second_layer(e - 1, 1 - b, NTB - 1)
            expert_steps(pe, expert)
            second_layer(E - 1, 1, NTB - 1)

        @block.scalar
        def _(act):
            def prep(items, first):
                n = len(items)
                for s in range(n + 1):
                    if s < n:
                        i, w = first + s, items[s][3]
                        act.wait_ge(s_q, i + 1)
                        if i >= 3:
                            act.wait_ge(s_st[i % 3], 16 * (i // 3))
                        act.activation(parts[:, i % 3, 0, 0:w], QF[:, i % 3, 0:w], ACT.Copy).then_inc(s_hi, 1)
                    if s >= 1:
                        i, w = first + s - 1, items[s - 1][3]
                        act.wait_ge(s_r, i + 1)
                        act.activation(parts[:, i % 3, 1, 0:w], RF[:, i % 2, 0:w], ACT.Copy).then_inc(s_mi, 1)

            def v_save(V, n, first):
                for t in range(n):
                    i = first + t
                    act.wait_ge(s_v, i + 1)
                    act.activation(V[:, t, :], B[4 + i % 2][:, 0:C], ACT.Copy).then_inc(s_vs, 1)

            prep(PREP1[0:16], 0)
            v_save(VA, TT, 0)
            prep(PREP1[16:], 16)
            v_save(VX, NXP // P, TT)

            def attention(A, plan):
                def save(q, h):
                    act.wait_ge(A.pv, plan.nb * h + (plan.last_batch[q] + 1))
                    if not (isinstance(h, int) and h == 0 and q < 2):
                        act.wait_ge(A.sums, h * NQB + (q - 1))
                    act.activation(OS[:, q % 2, :], O[q % 2][:, :], ACT.Copy).then_inc(A.saved, 1)

                def step(h, c, turn):
                    first = isinstance(h, int) and h == 0
                    for b in range(plan.nb):
                        for u in range(4 * b, 4 * b + 4):
                            act.wait_ge(A.scores, plan.nu * h + (u + 1))
                            if u % 4 == 0 and not (first and u < PRING):
                                act.wait_ge(A.pv, plan.nb * h + (b - PRING // 4 + 1))
                            act.activation(PT[:, (c * plan.nu + u) % PRING, :], S[(c * plan.nu + u) % SBANKS][:, :],
                                           ACT.Exp).then_inc(A.exps, 1)
                            if u % 4 == 1:
                                for q, back in plan.saves(b, first):
                                    save(q, h + back)
                head_steps(act, step)
                for q in range(NQB):
                    if plan.last_batch[q] + 2 >= plan.nb:
                        save(q, H - 1)

            def root(i):
                act.wait_ge(s_var, i + 1)
                act.activation(var[:, i % 2, 1:2], var[:, i % 2, 0:1], ACT.Sqrt).then_inc(s_sd, 1)

            def transposes(call):
                b0 = call * TT
                for s in range(TT + 3):
                    if s < TT:
                        act.wait_ge(s_tr, b0 + s + 1)
                        if s >= 2:
                            act.wait_ge(s_pj, b0 + s - 1)
                        act.activation(ATT[:, s % 2, :, :].rearrange("p k j -> p (k j)"), B[s % 2][:, 0:C],
                                       ACT.Copy).then_inc(s_att, 1)
                    if 1 <= s <= TT:
                        root(b0 + s - 1)
                    t = s - 3
                    if t >= 0:
                        act.wait_ge(s_xt, b0 + t + 1)
                        act.activation(XT[:, :, t * P:(t + 1) * P], O[t % 2][:, 0:C].rearrange("p (k j) -> p k j", k=CT),
                                       ACT.Copy).then_inc(s_xts, 1)

            attention(SA, SELF)
            transposes(0)
            prep(PREP2, NPREP)
            attention(XA, CROSS)
            transposes(1)
            act.wait_ge(s_gc, 2)
            act.activation(G[:, :, :], cmp_[:, :, :], ACT.Exp).then_inc(s_ge, 1)
            act.wait_ge(s_gt, 1)
            for j in range(4):
                act.activation(GT[:, j * QB:(j + 1) * QB], B[j][0:E, :], ACT.Copy).then_inc(s_gts, 1)
            def expert(e, b):
                act.activation(b1E[:, b, :], b1S[:, bass.ds(e * FT, FT)], ACT.Copy).then_inc(s_b1, 1)
                act.wait_ge(s_b1, e + 1)
                for blk in range(NTB):
                    for i in range(PB):
                        pair = blk * PB + i
                        act.wait_ge(s_hid, e * (NTB * PB) + (pair + 1))
                        if not (isinstance(e, int) and e == 0 and pair < PB):
                            act.wait_ge(s_hs, e * (NTB * PB) + (pair + 1 - PB))
                        for q in range(2):
                            ins = act.activation(GR[:, i, q, :], B[i][:, q * TB:(q + 1) * TB], ACT.Gelu,
                                                 bias=b1E[:, b, 2 * i + q:2 * i + q + 1])
                        ins.then_inc(s_gelu, 1)
            expert_steps(act, expert)
            for t in range(TT):
                root(2 * TT + t)

        @block.vector
        def _(dve):
            links = {}

            def link(ins, s):
                links[s] = links.get(s, 0) + 1
                ins.then_inc(s, 1)
                dve.wait_ge(s, links[s])

            def prep(items, first):
                n = len(items)
                for s in range(n + 2):
                    if s < n:
                        i = first + s
                        kind, half, c0, w = items[s]
                        dve.wait_ge(s_prep, i + 1)
                        if i >= 3:
                            dve.wait_ge(s_r, i - 2)
                        if kind in "qk":
                            if i >= 2:
                                dve.wait_ge(s_q, i - 1)
                            dve.tensor_tensor(T1[:, i % 2, 0:w], B[2 * (i % 2)][:, 0:w], cosS[:, c0:c0 + w], ALU.mult)
                            ins = dve.tensor_tensor(T2[:, i % 2, 0:w], B[2 * (i % 2) + 1][:, 0:w], sinS[:, c0:c0 + w], ALU.mult)
                            ins.then_inc(s_prepfree, 1)
                            dve.wait_ge(s_prepfree, i + 1)
                            dve.tensor_tensor(QF[:, i % 3, 0:w], T1[:, i % 2, 0:w], T2[:, i % 2, 0:w], ALU.add).then_inc(s_q, 1)
                        else:
                            dve.tensor_scalar(QF[:, i % 3, 0:w], B[2 * (i % 2)][:, 0:w], SCALE if kind == "xq" else 1.0, None,
                                              ALU.mult).then_inc(s_prepfree, 1)
                            dve.wait_ge(s_prepfree, i + 1)
                            dve.sem_inc(s_q, 1)
                    if 1 <= s <= n:
                        i, w = first + s - 1, items[s - 1][3]
                        dve.wait_ge(s_hi, i + 1)
                        if i >= 2:
                            dve.wait_ge(s_lo, i - 1)
                        dve.tensor_tensor(RF[:, i % 2, 0:w], QF[:, i % 3, 0:w], parts[:, i % 3, 0, 0:w], ALU.subtract).then_inc(s_r, 1)
                    if s >= 2:
                        i, w = first + s - 2, items[s - 2][3]
                        dve.wait_ge(s_mi, i + 1)
                        dve.tensor_tensor(parts[:, i % 3, 2, 0:w], RF[:, i % 2, 0:w], parts[:, i % 3, 1, 0:w], ALU.subtract).then_inc(s_lo, 1)

            dve.wait_ge(s_rope, 32)
            prep(PREP1[0:16], 0)

            dve.wait_ge(s_k, 16 * 9)
            link(dve.memset(slopeF, 1.0), s_chain)
            link(dve.memset(SHW[:, :], 0.0), s_chain)
            link(dve.tensor_scalar(slRow[:, 1:2], slRow[:, 0:1], MAX_BIAS, None, ALU.mult), s_chain)
            link(dve.tensor_copy(slRowB[:, 0:1], slRow[:, 1:2]), s_chain)
            link(dve.tensor_tensor(slRow[:, 2:3], slRow[:, 1:2], slRowB[:, 0:1], ALU.subtract), s_chain)
            link(dve.tensor_copy(slRowB[:, 1:2], slRow[:, 2:3]), s_chain)
            link(dve.tensor_tensor(slRowB[:, 2:3], slRow[:, 2:3], slRowB[:, 1:2], ALU.subtract), s_chain)
            link(dve.tensor_tensor(slRow[:, 3:6], slRowB[:, 0:3], pickS[:, :], ALU.mult), s_chain)
            link(dve.tensor_reduce(slRow[:, 6:7], slRow[:, 3:6], AX.X, ALU.add), s_chain)
            dve.tensor_scalar(slopeF, slopeF, slRow[:, 6:7], None, ALU.mult).then_inc(s_sl, 1)
            link(dve.tensor_scalar(sl8[:, :], slB[:, :], MAX_BIAS, None, ALU.mult), s_chain)
            link(dve.tensor_copy(slP[:, 0, :], sl8[:, :]), s_chain)
            link(dve.tensor_tensor(slR[:, :], sl8[:, :], slP[:, 0, :], ALU.subtract), s_chain)
            link(dve.tensor_copy(slP[:, 1, :], slR[:, :]), s_chain)
            link(dve.tensor_tensor(slP[:, 2, :], slR[:, :], slP[:, 1, :], ALU.subtract), s_chain)
            link(dve.tensor_copy(slPF[:, :, :], slP[:, :, :]), s_chain)
            for h in range(H):
                if h >= 2:
                    dve.wait_ge(s_sdo[h % 2], 16 * (h // 2))
                for s in range(PARTS):
                    ins = dve.tensor_scalar(slopeDiag[:, h % 2, s, :], idf[:, :], slPF[:, s, h:h + 1], None, ALU.mult)
                ins.then_inc(s_sdr, 1)
            link(dve.memset(mRow[:, :], MASKED), s_mask)
            dve.tensor_scalar(mRow[:, 0:NX], mU8[:, :], -1.0, -MASKED, ALU.add, ALU.mult).then_inc(s_mask, 1)
            dve.wait_ge(s_m, 16 * 5)
            link(dve.tensor_tensor(X[:, :, :], X[:, :, :], bpS[:, :].unsqueeze(1).to_broadcast([P, TT, C]), ALU.add), s_chain)


            prep(PREP1[16:], 16)

            def attention(A, plan):
                ch = plan.chunk

                def ring_item(item, pos, bank, h):
                    kind, a, b, ahead = item
                    slot = R[bank % RBANKS]
                    if kind == "max":
                        dve.wait_ge(A.filled, pos + 1)
                        dve.tensor_reduce(CM[:, a, b:b + 1], slot[:, 0:ch], AX.X, ALU.max).then_inc(A.freed, 1)
                        if (a, b) == (TT - 1, 3):
                            n = (h + ahead) * 4
                            dve.wait_ge(A.freed, pos + 1)
                            dve.tensor_reduce(NM[:, :], CM[:, :, :], AX.X, ALU.max, negate=True).then_inc(A.chain, 1)
                            dve.wait_ge(A.chain, n + 1)
                            dve.tensor_copy(SH[:, 0, :], NM[:, :]).then_inc(A.chain, 1)
                            dve.wait_ge(A.chain, n + 2)
                            dve.tensor_tensor(NR[:, :], NM[:, :], SH[:, 0, :], ALU.subtract).then_inc(A.chain, 1)
                            dve.wait_ge(A.chain, n + 3)
                            dve.tensor_copy(SH[:, 1, :], NR[:, :]).then_inc(A.chain, 1)
                            dve.wait_ge(A.chain, n + 4)
                            dve.tensor_tensor(SH[:, 2, :], NR[:, :], SH[:, 1, :], ALU.subtract).then_inc(A.cols, 1)
                    elif kind == "shift":
                        dve.wait_ge(A.filled, pos + 1)
                        if not (isinstance(h, int) and h < 0):
                            dve.wait_ge(A.shift_loaded, (h + 1) * (16 * PARTS))
                        dve.tensor_copy(MT[:, :], slot[0:PARTS * TT, 0:P // 2].bitcast(BF16)).then_inc(A.freed, 1)
                    else:
                        dve.wait_ge(A.filled, pos + 1)
                        g = (h + ahead) * NQB + a
                        v = slot[:, 0:P].rearrange("p (t j) -> p t j", j=32)
                        dve.reciprocal(RC[:, a % 2, :, :], v[:, :, D:D + 1]).then_inc(A.sums, 1)
                        dve.wait_ge(A.sums, g + 1)
                        dve.tensor_tensor(AT[:, 4 * a:4 * a + 4, bass.ds((h + ahead) * D, D)], v[:, :, 0:D],
                                          RC[:, a % 2, :, :].to_broadcast([P, 4, D]), ALU.mult).then_inc(A.freed, 1)

                def step(h, c, turn):
                    whole = isinstance(h, int)
                    first = whole and h == 0
                    pos, bank, off = plan.ring_before(h), plan.static_before(h, c), 0
                    for b in range(plan.nb):
                        for item in plan.ring_items(b, h):
                            ring_item(item, pos + off, bank + off, h)
                            off += width(item)
                pos = 0
                for item in plan.prologue:
                    ring_item(item, pos, pos, -1)
                    pos += width(item)
                head_steps(dve, step)
                end = plan.ring_before(H)
                for q in plan.tail:
                    ring_item(("sum", q, 0, 0), end, end, H - 1)
                    end += 1

            def norms(call):
                for s in range(TT + 1):
                    if s < TT:
                        b = s % 2
                        y = X[:, s, :] if call < 2 else AT[:, s, :]
                        if call < 2:
                            dve.wait_ge(s_pj, call * TT + s + 1)
                            link(dve.tensor_tensor(y, B[2 + b][:, 0:C], y, ALU.add), s_ln)
                        link(dve.bn_stats(stats[:, b, :], y), s_ln)
                        link(dve.bn_aggr(agg[:, b, :], stats[:, b, :]), s_ln)
                        dve.tensor_scalar(var[:, b, 0:1], agg[:, b, 1:2], EPS, None, ALU.add).then_inc(s_var, 1)
                    if s >= 1:
                        t, b = s - 1, (s - 1) % 2
                        y = X[:, t, :] if call < 2 else AT[:, t, :]
                        dve.wait_ge(s_sd, call * TT + t + 1)
                        link(dve.reciprocal(var[:, b, 2:3], var[:, b, 1:2]), s_ln)
                        link(dve.scalar_tensor_tensor(out=var[:, b, 3:4], in0=var[:, b, 2:3], scalar=var[:, b, 2:3],
                                                      in1=var[:, b, 0:1], op0=ALU.mult, op1=ALU.mult), s_ln)
                        link(dve.tensor_scalar(var[:, b, 3:4], var[:, b, 3:4], -0.5, 1.5, ALU.mult, ALU.add), s_ln)
                        link(dve.tensor_tensor(var[:, b, 4:5], var[:, b, 2:3], var[:, b, 3:4], ALU.mult), s_ln)
                        dve.tensor_scalar(X[:, t, :], y, agg[:, b, 0:1], var[:, b, 4:5], ALU.subtract, ALU.mult).then_inc(s_xn, 1)

            attention(SA, SELF)
            norms(0)
            prep(PREP2, NPREP)
            attention(XA, CROSS)
            norms(1)

            gc = [0]

            def glink(ins):
                gc[0] += 1
                ins.then_inc(s_gc, 1)
                dve.wait_ge(s_gc, gc[0])
            dve.wait_ge(s_log, 1)
            dve.tensor_copy(L[:, :, :], B[4][:, 0:TT * E].rearrange("p (t e) -> p t e", e=E)).then_inc(s_gl, 1)
            dve.wait_ge(s_gl, 1)
            glink(dve.tensor_reduce(top[:, :, 0], L[:, :, :], AX.X, ALU.max))
            glink(dve.tensor_tensor(cmp_[:, :, :], L[:, :, :], top[:, :, :].to_broadcast([P, TT, E]), ALU.subtract))
            glink(dve.memset(rank[:, :, :], 0.0))
            for j in range(E):
                lj = L[:, :, j:j + 1]
                if j + 1 < E:
                    glink(dve.tensor_tensor(beat[:, :, j + 1:E], lj.to_broadcast([P, TT, E - 1 - j]), L[:, :, j + 1:E], ALU.is_ge))
                glink(dve.tensor_tensor(beat[:, :, 0:j + 1], lj.to_broadcast([P, TT, j + 1]), L[:, :, 0:j + 1], ALU.is_gt))
                glink(dve.tensor_tensor(rank[:, :, :], rank[:, :, :], beat[:, :, :], ALU.add))
            glink(dve.tensor_scalar(rank[:, :, :], rank[:, :, :], 2.0, None, ALU.is_lt))
            dve.wait_ge(s_ge, 1)
            glink(dve.tensor_tensor(G[:, :, :], G[:, :, :], rank[:, :, :], ALU.mult))
            glink(dve.tensor_reduce(top[:, :, 0], G[:, :, :], AX.X, ALU.add))
            glink(dve.reciprocal(top[:, :, :], top[:, :, :]))
            dve.tensor_tensor(G[:, :, :], G[:, :, :], top[:, :, :].to_broadcast([P, TT, E]), ALU.mult).then_inc(s_g, 1)

            for t in range(TT):
                dve.wait_ge(s_b2, t + 1)
                dve.tensor_tensor(AT[:, t, :], O[t % 2][:, 0:C], X[:, t, :], ALU.add).then_inc(s_acc0, 1)
            dve.wait_ge(s_acc0, TT)
            dve.wait_ge(s_g, 1)
            def add_block(e, blk):
                for j in range(2):
                    m = 2 * blk + j
                    dve.wait_ge(s_moe, e * TT + (m + 1))
                    dve.scalar_tensor_tensor(out=AT[:, m, :], in0=B[4 + m % 4][:, 0:C], scalar=G[:, m, bass.ds(e, 1)],
                                             in1=AT[:, m, :], op0=ALU.mult, op1=ALU.add).then_inc(s_moef, 1)

            def expert(e, b):
                whole = isinstance(e, int)
                for blk in range(NTB):
                    for i in range(PB):
                        pair = blk * PB + i
                        dve.wait_ge(s_gelu, e * (NTB * PB) + (pair + 1))
                        if i == 0 and not (whole and e == 0 and blk < 2):
                            dve.wait_ge(s_moe, e * TT + (2 * blk - 2))
                        hi = HH[:, blk % 2, 2 * i:2 * i + 2, :]
                        dve.tensor_copy(hi, GR[:, i, :, :]).then_inc(s_hh, 1)
                        dve.wait_ge(s_hh, e * (NTB * PB) + (pair + 1))
                        dve.tensor_tensor(HL[:, blk % 2, 2 * i:2 * i + 2, :], GR[:, i, :, :], hi.bitcast(F32),
                                          ALU.subtract).then_inc(s_hs, 1)
                    if blk:
                        add_block(e, blk - 1)
                    elif not (whole and e == 0):
                        add_block(e - 1, NTB - 1)
                    if not (whole and e == E - 1):
                        if blk == 0:
                            dve.wait_ge(s_raw, e * 32 + 64)
                        for n in {0: (0, 1), NTB - 1: ()}.get(blk, (blk + 1,)):
                            w = slice(n * PIECE, (n + 1) * PIECE)
                            dve.tensor_copy(WH[:, 1 - b, w], WR[:, w]).then_inc(s_wh, 1)
                            dve.wait_ge(s_wh, e * NPIECE + (n + 1))
                            dve.tensor_tensor(WL[:, 1 - b, w], WR[:, w], WH[:, 1 - b, w].bitcast(F32),
                                              ALU.subtract).then_inc(s_ws, 1)
            expert_steps(dve, expert)
            add_block(E - 1, NTB - 1)
            dve.wait_ge(s_moef, E * TT)
            norms(2)


def _tables():
    def bf(v):
        return (np.ascontiguousarray(v, dtype=np.float32).view(np.uint32) >> 16).astype(np.uint16)
    pos = np.arange(N)
    inv = (np.float32(1.0) / np.float32(10000.0) ** (np.arange(0, D, 2, dtype=np.float32) / np.float32(D))).astype(np.float32)
    freqs = (pos.astype(np.float32)[:, None] * inv[None, :]).astype(np.float32)
    cos, sin = np.cos(freqs).T, np.sin(freqs).T
    root = np.float32(SCALE ** 0.5)
    cosT = np.tile(np.concatenate([cos, cos]), (P // D, 1)).astype(np.float32) * root
    sinT = np.tile(np.concatenate([-sin, sin]), (P // D, 1)).astype(np.float32) * root
    hi, lo = pos // P * P, pos % P
    q = np.zeros((S0, N), np.float32)
    kl = np.zeros((S0, N), np.float32)
    for s in range(PARTS):
        q[4 * s + 1], q[4 * s + 3] = -hi, -lo
        kl[4 * s], kl[4 * s + 2] = hi, lo
    q[MASK_ROW] = 1.0
    qx = np.zeros((S0, N), np.float32)
    qx[MASK_ROW] = 1.0
    sel = np.zeros((P, D + 2), np.float32)
    for g in range(4):
        sel[32 * g + np.arange(D + 1), np.arange(D + 1)] = 1.0
    j = np.arange(P)
    dist = np.minimum(j[None, :] - j[:, None], 0)
    pick = np.zeros((6 * H, PARTS), np.float32)
    pick[np.arange(6 * H), np.arange(6 * H) % 6 // 2] = 1.0
    return {
        "cosT": cosT, "sinT": sinT, "constQ": bf(q), "constQX": bf(qx), "constKL": bf(kl),
        "constK0": bf(np.zeros((S0, N))), "ones3": bf(np.ones((PARTS, N))), "ident": np.eye(P, dtype=np.float32),
        "identb": bf(np.eye(P)), "dist": bf(dist), "distT": bf(dist.T), "sel": sel, "pick": pick,
    }


def kernel(**inputs):
    import concourse.bacc as _bacc
    from concourse.bass_utils import run_bass_kernel_spmd as _run

    i = {k: np.asarray(v) for k, v in inputs.items()}
    qkv = i["L0_attn_qkv_w"]
    rot = np.arange(2 * C).reshape(-1, 2, D // 2)[:, ::-1].reshape(-1)
    a = {
        "x": i["x"][0], "xT": i["x"][0].T, "ctxT": i["ctx_1024"][0].T,
        "mask": i["mask_Bx1x1xS2_bf1"].reshape(1, NX).view(np.uint8),
        "wqkvT": qkv.T, "wrotT": qkv[rot].T, "wpT": i["L0_attn_proj_w"].T, "bp": i["L0_attn_proj_b"],
        "slopes": i["L0_attn_slopes"], "xwqT": i["L0_xattn_Wq"].T, "xwkT": i["L0_xattn_Wk"].T,
        "xwvT": i["L0_xattn_Wv"].T, "xwoT": i["L0_xattn_Wo"].T, "rT": i["L0_ffn_router_w"].T,
        "w1T": i["L0_ffn_w1"].transpose(0, 2, 1).reshape(E * C, F),
        "b1T": i["L0_ffn_b1"].reshape(E * FT, P).T,
        "w2T": i["L0_ffn_w2"].transpose(0, 2, 1).reshape(E * F, C), "b2": i["L0_ffn_b2"],
    }
    a.update(_tables())
    nc = _bacc.Bacc("TRN2", target_bir_lowering=False, num_devices=1)
    arrays, aps = {}, {}
    for name, v in a.items():
        v = np.ascontiguousarray(v)
        arrays[f"in_{name}_dram"] = v
        aps[name] = nc.dram_tensor(f"in_{name}_dram", v.shape, mybir.dt.from_np(v.dtype), kind="ExternalInput").ap()
        if v.dtype == np.uint16:
            aps[name] = aps[name].bitcast(BF16)
    aps["out"] = nc.dram_tensor("out_0_dram", (1, N, C), F32, kind="ExternalOutput").ap().rearrange("o n c -> (o n) c")
    layer(nc, **aps)
    r = _run(nc, [arrays], core_ids=[0])
    return r.results[0]["out_0_dram"]
```
